# Optimizing a Trainium2 kernel written in Bass

```python
import numpy as np
import jax
import jax.numpy as jnp

def _softmax(x, axis=-1):
    return jax.nn.softmax(x, axis=axis)

def _gelu(x):
    return jax.nn.gelu(x, approximate=True)

def _silu(x):
    return jax.nn.silu(x)

def _sigmoid(x):
    return jax.nn.sigmoid(x)

def _layernorm(x, axis=-1, eps=1e-05):
    m = jnp.mean(x, axis=axis, keepdims=True)
    v = jnp.var(x, axis=axis, keepdims=True)
    return (x - m) / jnp.sqrt(v + eps)

def _scatter_add(tgt, idx, src, axis=0):
    return tgt.at[idx].add(src)

def _segment_sum(src, seg, n):
    return jax.ops.segment_sum(src, seg, n)
kernel_name = 'mk_xattn_seq_d1_seqx_r2_0a0028'

def setup_inputs(seed: int=0):
    np.random.seed(seed)
    _w = jnp.asarray

    def _rec_inputs():
        import jax
        import jax.numpy as jnp
        _rk = jax.random.key(seed)
        x = -0.0002928 + 1 * jax.random.normal(jax.random.fold_in(_rk, 1), (16, 512, 512), jnp.float32)
        _lenS = 512 - jax.random.randint(jax.random.fold_in(_rk, 7), (16,), 0, max(1, 512 // 4) + 1, jnp.int32)
        _lenS2 = 77 - jax.random.randint(jax.random.fold_in(_rk, 8), (16,), 0, max(1, 77 // 4) + 1, jnp.int32)
        _ctx_1024P = jax.random.normal(jax.random.fold_in(_rk, 11), (16, 16, 512), jnp.float32)
        _ctx_1024c = jax.random.dirichlet(jax.random.fold_in(_rk, 511), 0.3 * jnp.ones((16,), jnp.float32), (16, 77))
        _ctx_1024t = jnp.einsum('bsk,bkd->bsd', _ctx_1024c, _ctx_1024P)
        _ctx_1024t = _ctx_1024t * jax.lax.rsqrt(jnp.mean(jnp.square(_ctx_1024t)) + 1e-12) * 0.953939
        ctx_1024 = -1.39393e-06 + 0.999914 * (_ctx_1024t + 0.3 * jax.random.normal(jax.random.fold_in(_rk, 611), (16, 77, 512), jnp.float32))
        return (x, ctx_1024)
    x, ctx_1024 = _rec_inputs()

    def _L0_xattn_setup():
        import jax, jax.numpy as jnp
        import numpy as np
        D_MODEL = 512
        NUM_HEADS = 16
        D_K = D_MODEL // NUM_HEADS

        def _layer_norm(x, gamma, beta, eps=1e-05):
            mu = jnp.mean(x, axis=-1, keepdims=True)
            var = jnp.mean(jnp.square(x - mu), axis=-1, keepdims=True)
            return (x - mu) * jax.lax.rsqrt(var + eps) * gamma + beta
        key = jax.random.key(seed)
        ks = jax.random.split(key, 12)
        B, S = (2, 1024)
        s = 1.0 / np.sqrt(D_MODEL)
        inp = {'query': jax.random.normal(ks[0], (B, S, D_MODEL), jnp.float32), 'key': jax.random.normal(ks[1], (B, S, D_MODEL), jnp.float32), 'value': jax.random.normal(ks[2], (B, S, D_MODEL), jnp.float32), 'Wq': jax.random.normal(ks[3], (D_MODEL, D_MODEL), jnp.float32) * s, 'bq': jnp.zeros((D_MODEL,), jnp.float32), 'Wk': jax.random.normal(ks[4], (D_MODEL, D_MODEL), jnp.float32) * s, 'bk': jnp.zeros((D_MODEL,), jnp.float32), 'Wv': jax.random.normal(ks[5], (D_MODEL, D_MODEL), jnp.float32) * s, 'bv': jnp.zeros((D_MODEL,), jnp.float32), 'Wo': jax.random.normal(ks[6], (D_MODEL, D_MODEL), jnp.float32) * s, 'bo': jnp.zeros((D_MODEL,), jnp.float32), 'ln_gamma': jnp.ones((D_MODEL,), jnp.float32), 'ln_beta': jnp.zeros((D_MODEL,), jnp.float32)}
        return inp
    _L0_xattn_all = _L0_xattn_setup()
    _L0_xattn_in = {k: v for k, v in _L0_xattn_all.items() if k in ('Wq', 'bq', 'Wk', 'bk', 'Wv', 'bv', 'Wo', 'bo', 'ln_gamma', 'ln_beta')}
    del _L0_xattn_all
    return {'x': x, 'ctx_1024': ctx_1024, 'L0_xattn_Wq': _L0_xattn_in['Wq'], 'L0_xattn_bq': _L0_xattn_in['bq'], 'L0_xattn_Wk': _L0_xattn_in['Wk'], 'L0_xattn_bk': _L0_xattn_in['bk'], 'L0_xattn_Wv': _L0_xattn_in['Wv'], 'L0_xattn_bv': _L0_xattn_in['bv'], 'L0_xattn_Wo': _L0_xattn_in['Wo'], 'L0_xattn_bo': _L0_xattn_in['bo'], 'L0_xattn_ln_gamma': _L0_xattn_in['ln_gamma'], 'L0_xattn_ln_beta': _L0_xattn_in['ln_beta']}

def reference(x, ctx_1024, L0_xattn_Wq, L0_xattn_bq, L0_xattn_Wk, L0_xattn_bk, L0_xattn_Wv, L0_xattn_bv, L0_xattn_Wo, L0_xattn_bo, L0_xattn_ln_gamma, L0_xattn_ln_beta):
    import jax
    import jax.numpy as jnp

    def _L0_xattn_ref(query, key, value, Wq, bq, Wk, bk, Wv, bv, Wo, bo, ln_gamma, ln_beta):
        import jax, jax.numpy as jnp
        import numpy as np
        D_MODEL = 512
        NUM_HEADS = 16
        D_K = D_MODEL // NUM_HEADS

        def _layer_norm(x, gamma, beta, eps=1e-05):
            mu = jnp.mean(x, axis=-1, keepdims=True)
            var = jnp.mean(jnp.square(x - mu), axis=-1, keepdims=True)
            return (x - mu) * jax.lax.rsqrt(var + eps) * gamma + beta
        B, S, _ = query.shape

        def split_heads(x):
            return x.reshape(B, -1, NUM_HEADS, D_K).transpose(0, 2, 1, 3)
        Q = split_heads(query @ Wq + bq)
        K = split_heads(key @ Wk + bk)
        V = split_heads(value @ Wv + bv)
        scores = jnp.einsum('bhqd,bhkd->bhqk', Q, K) / np.sqrt(D_K).astype(np.float32)
        attn = jax.nn.softmax(scores, axis=-1)
        ctx = jnp.einsum('bhqk,bhkd->bhqd', attn, V)
        ctx = ctx.transpose(0, 2, 1, 3).reshape(B, S, D_MODEL)
        out = ctx @ Wo + bo
        return _layer_norm(out + query, ln_gamma, ln_beta)
    x = _L0_xattn_ref(x, ctx_1024, ctx_1024, L0_xattn_Wq, L0_xattn_bq, L0_xattn_Wk, L0_xattn_bk, L0_xattn_Wv, L0_xattn_bv, L0_xattn_Wo, L0_xattn_bo, L0_xattn_ln_gamma, L0_xattn_ln_beta)
    return x

_drawn_inputs = setup_inputs


def setup_inputs(seed=0):
    import zlib

    import numpy as np

    out = dict(_drawn_inputs(seed))
    spreads = {'L0_xattn_bq': (0.0, 0.397),
     'L0_xattn_bk': (0.0, 0.8),
     'L0_xattn_bv': (0.0, 0.1),
     'L0_xattn_bo': (0.0, 0.1),
     'L0_xattn_ln_gamma': (1.0, 0.2),
     'L0_xattn_ln_beta': (0.0, 0.1)}
    factors = {}
    for name, (base, spread) in spreads.items():
        noise = np.random.default_rng([zlib.crc32(name.encode()), seed]).standard_normal(out[name].shape)
        drawn = base * np.exp(spread * noise) if base else spread * noise
        out[name] = jnp.asarray(drawn.astype(out[name].dtype))
    for name, factor in factors.items():
        out[name] = (out[name] * factor).astype(out[name].dtype)
    return out
```

```python
from contextlib import ExitStack

import concourse.bass as bass
from concourse import mybir

F32 = mybir.dt.float32
F32R = mybir.dt.float32r
ALU = mybir.AluOpType
ACT = mybir.ActivationFunctionType
AX_X = mybir.AxisListType.X

P = 128
D = 512
KC = D // P
DK = 32
HC = P // DK
NCH = D // P
HALF = 2 * HC
PAIR = 2 * NCH
EPS = 1e-5

LAG_SPLIT = -4
LAG_LOAD_X = -5
LAG_ROWMAX = 1
LAG_PV = 5
LAG_SCORE = 4
LAG_OUT = 9
LAG_NORM = 10
LAG_SCALE = 11
LAG_STORE = 12


class Slot:

    def __init__(self, u, k):
        self.u, self.k = u, k

    def back(self, lag):
        return Slot(self.u, self.k - lag)

    def over(self, d, plus=0, times=1):
        return self.u * (PAIR // d * times) + (self.k // d + plus) * times

    def valid(self, n):
        return not isinstance(self.u, int) or 0 <= PAIR * self.u + self.k < n


def at_least(engine, sem, value):
    if not isinstance(value, int) or value > 0:
        engine.wait_ge(sem, value)


def all_at_least(engine, *waits):
    for _, value in waits:
        if not isinstance(value, int):
            engine.compute_val(value)
    for sem, value in waits:
        at_least(engine, sem, value)


def project_context(nc, a, keep, kh_dram, kl_dram, v_dram, B, S2):
    NK = B * S2
    NT = 3
    cuts = [0] + [(NK * (i + 1) // NT + 1) // 2 * 2 for i in range(NT - 1)] + [NK]
    tiles_k = [(c, cuts[i], cuts[i + 1]) for c in range(KC) for i in range(NT)]
    tiles_v = [(r, min(P, NK - r)) for r in range(0, NK, P)]
    with ExitStack() as ctx:
        def sb(name, shape, dt):
            return ctx.enter_context(nc.sbuf_tensor(name, shape, dt))

        def sem(name):
            return ctx.enter_context(nc.semaphore(name))

        cx = sb("cx", [P, KC, NK], F32)
        cxh, cxl = sb("cxh", [P, KC, NK], F32R), sb("cxl", [P, KC, NK], F32R)
        w_raw = {n: sb(f"w{n}_raw", [P, KC, D], F32) for n in "kvqo"}
        wkh, wkl = sb("wkh", [P, KC, D], F32R), sb("wkl", [P, KC, D], F32R)
        wvh, wvl = sb("wvh", [P, KC, D], F32R), sb("wvl", [P, KC, D], F32R)
        kth, ktl = sb("kth", [P, 2, NK], F32R), sb("ktl", [P, 2, NK], F32R)
        vt = sb("vt", [P, 2, D], F32)
        bv_row = sb("bv_row", [P, D], F32)
        bk_col = sb("bk_col", [P, KC], F32)
        pk = [ctx.enter_context(nc.psum_tensor(f"pk{i}", [P, D], F32)) for i in range(4)]
        pv = [ctx.enter_context(nc.psum_tensor(f"pvv{i}", [P, D], F32)) for i in range(2)]

        loaded = [sem(f"loaded_{n}") for n in ("cx", "wk", "wv", "wq", "wo")]
        biases_in = sem("biases_in")
        high_ready, low_ready = sem("high_ready"), sem("low_ready")
        k_summed, k_high_out, k_low_out = sem("k_summed"), sem("k_high_out"), sem("k_low_out")
        v_summed, v_out = sem("v_summed"), sem("v_out")
        k_stored = [sem(f"k_stored{i}") for i in range(2)]
        v_stored = [sem(f"v_stored{i}") for i in range(2)]
        splits = [(cx, cxh, cxl), (w_raw["k"], wkh, wkl), (w_raw["v"], wvh, wvl),
                  (w_raw["q"], keep["wqh"], keep["wql"]), (w_raw["o"], keep["woh"], keep["wol"])]
        with nc.Block() as block:
            @block.sync
            def _(sp):
                sp.dma_start(cx[:], a["ctx_t"].rearrange("(c p) n -> p c n", p=P)).then_inc(loaded[0], 16)
                for i, n in enumerate("kvqo"):
                    sp.dma_start(w_raw[n][:], a["W" + n].rearrange("(c p) n -> p c n", p=P)).then_inc(loaded[1 + i], 16)
                    if i == 0:
                        sp.dma_start(bk_col[:], a["bk"]).then_inc(biases_in, 16)
                        sp.dma_start(bv_row[:], a["bv"].partition_broadcast(P)).then_inc(biases_in, 16)
                for c in range(KC):
                    sp.wait_ge(k_high_out, NT * (c + 1))
                    sp.wait_ge(k_low_out, NT * (c + 1))
                    for t, dst in ((kth, kh_dram), (ktl, kl_dram)):
                        sp.dma_start(dst[:, P * c:P * (c + 1), :].rearrange("b p k -> p b k"),
                                     t[:, c % 2, :].bitcast(F32).rearrange("p (b k) -> p b k", k=S2)
                                     ).then_inc(k_stored[c % 2], 16)
                for i, (r, n) in enumerate(tiles_v):
                    sp.wait_ge(v_out, i + 1)
                    sp.dma_start(v_dram[r:r + n, :], vt[0:n, i % 2, :]).then_inc(v_stored[i % 2], 16)
                for i in range(2):
                    sp.wait_ge(k_stored[i], 16 * KC)
                    sp.wait_ge(v_stored[i], 16 * ((len(tiles_v) + 1 - i) // 2))

            @block.scalar
            def _(act):
                def split_high(i):
                    act.wait_ge(loaded[i], 16)
                    for c in range(KC):
                        nc.scalar.copy(splits[i][1][:, c, :], splits[i][0][:, c, :]).then_inc(high_ready, 1)
                for i in range(2):
                    split_high(i)
                act.wait_ge(biases_in, 32)
                for i, (c, lo, hi) in enumerate(tiles_k):
                    act.wait_ge(k_summed, i + 1)
                    if c >= 2:
                        act.wait_ge(k_stored[c % 2], 32)
                    nc.scalar.activation(kth[:, c % 2, lo:hi], pk[i % 4][:, 0:hi - lo], ACT.Identity,
                                         bias=bk_col[:, c:c + 1]).then_inc(k_high_out, 1)
                    if i in (1, 3, 5):
                        split_high(2 + i // 2)

            @block.vector
            def _(dve):
                def split_low(i):
                    for c in range(KC):
                        dve.wait_ge(high_ready, KC * i + c + 1)
                        nc.vector.tensor_tensor(splits[i][2][:, c, :], splits[i][0][:, c, :],
                                                splits[i][1][:, c, :].bitcast(F32), ALU.subtract).then_inc(low_ready, 1)
                for i in range(2):
                    split_low(i)
                dve.wait_ge(biases_in, 32)
                for i, (c, lo, hi) in enumerate(tiles_k):
                    dve.wait_ge(k_high_out, i + 1)
                    if c >= 2:
                        dve.wait_ge(k_stored[c % 2], 32)
                    nc.vector.scalar_tensor_tensor(
                        out=ktl[:, c % 2, lo:hi], in0=pk[i % 4][:, 0:hi - lo], scalar=bk_col[:, c:c + 1],
                        in1=kth[:, c % 2, lo:hi].bitcast(F32), op0=ALU.add, op1=ALU.subtract).then_inc(k_low_out, 1)
                    if i in (1, 3, 5):
                        split_low(2 + i // 2)
                for i, (r, n) in enumerate(tiles_v):
                    dve.wait_ge(v_summed, i + 1)
                    if i >= 2:
                        dve.wait_ge(v_stored[i % 2], 16 * (i // 2))
                    nc.vector.tensor_tensor(vt[0:n, i % 2, :], pv[i % 2][0:n, :], bv_row[0:n, :],
                                            ALU.add).then_inc(v_out, 1)

            @block.tensor
            def _(pe):
                for i, (c, lo, hi) in enumerate(tiles_k):
                    if i >= 4:
                        pe.wait_ge(k_low_out, i - 3)
                    for kc in range(KC):
                        if i == 0:
                            pe.wait_ge(low_ready, KC + kc + 1)
                        for n, (w, x) in enumerate(((wkh, cxh), (wkh, cxl), (wkl, cxh))):
                            last = nc.tensor.matmul(pk[i % 4][:, 0:hi - lo], w[:, kc, P * c:P * (c + 1)], x[:, kc, lo:hi],
                                                    start=(kc == 0 and n == 0), stop=(kc == KC - 1 and n == 2))
                    last.then_inc(k_summed, 1)
                pe.wait_ge(low_ready, 3 * KC)
                for i, (r, m) in enumerate(tiles_v):
                    if i >= 2:
                        pe.wait_ge(v_out, i - 1)
                    for kc in range(KC):
                        for n, (x, w) in enumerate(((cxh, wvh), (cxh, wvl), (cxl, wvh))):
                            last = nc.tensor.matmul(pv[i % 2][0:m, :], x[:, kc, r:r + m], w[:, kc, :],
                                                    start=(kc == 0 and n == 0), stop=(kc == KC - 1 and n == 2))
                    last.then_inc(v_summed, 1)


def attend(nc, a, keep, kh_dram, kl_dram, v_dram, out, B, S, S2):
    NG = B * NCH
    QT = S // P
    NM = B * QT
    assert QT == NCH and B % 2 == 0
    SCALE = float(DK) ** -0.5
    QI = 3 * DK
    KR = QI + HALF
    wqh, wql, woh, wol, bq_col = (keep[n] for n in ("wqh", "wql", "woh", "wol", "bq_col"))
    xt_dram = a["x_t"].rearrange("b (c p) s -> (b c) p s", p=P)
    x_dram = a["x"].rearrange("b (t p) d -> (b t) p d", p=P)
    out_dram = out.rearrange("b (t p) d -> (b t) p d", p=P)
    with ExitStack() as ctx:
        def sb(name, shape, dt):
            return ctx.enter_context(nc.sbuf_tensor(name, shape, dt))

        def psum(name):
            return ctx.enter_context(nc.psum_tensor(name, [P, 512], F32))

        def sem(name):
            return ctx.enter_context(nc.semaphore(name))

        xt = sb("xt", [P, 2, S], F32)
        xh, xl = (sb(n, [P, 2, KC, S], F32R) for n in ("xh", "xl"))
        qh, ql = (sb(n, [P, 2, 2, S], F32R) for n in ("qh", "ql"))
        z = sb("z", [P, 2, HALF, S], F32R)
        ks = sb("ks", [P, 2, NCH * HC, S2], F32R)
        kb = sb("kb", [P, 2, NCH, HC * S2], F32R)
        vb = sb("vb", [P, 2, D], F32)
        nm = sb("nm", [P, 2, QT, HALF], F32)
        prob = sb("prob", [P, HC, S], F32)
        rden = sb("rden", [P, S], F32)
        cx = sb("cxt", [P, 2, S], F32)
        ch, cl = (sb(n, [P, 2, KC, S], F32R) for n in ("ch", "cl"))
        xn = sb("xn", [P, 2, D], F32)
        y = sb("y", [P, 4, D], F32)
        stats = sb("stats", [P, 4, 6], F32)
        mv = sb("mv", [P, 4, 2], F32)
        ve, rstd, nmr = (sb(n, [P, 4, 1], F32) for n in ("ve", "rstd", "nmr"))
        minus_half = sb("minus_half", [P, 1], F32)
        ident = sb("ident", [P, P], F32)
        ones = sb("ones", [P, DK], F32)
        gamma, beta, bo = (sb(n, [P, D], F32) for n in ("gamma_row", "beta_row", "bo_row"))
        p_q, p_t, p_v, p_d, p_o = (psum(n) for n in ("p_q", "p_t", "p_v", "p_d", "p_o"))
        p_s = [psum(f"p_s{i}") for i in range(2)]
        p_a = [psum("p_a"), p_s[0]]

        xt_in = [sem(f"xt_in{i}") for i in range(2)]
        xn_in = [sem(f"xn_in{i}") for i in range(2)]
        kb_in = [sem(f"kb_in{i}") for i in range(2)]
        ksv_in = [sem(f"ksv_in{i}") for i in range(2)]
        z_in = [sem(f"z_in{i}") for i in range(2)]
        stored = [sem(f"stored{i}") for i in range(4)]
        rows_in = sem("rows_in")
        q_summed, a_summed, t_done, s_summed, pv_summed, o_summed = (
            sem(n) for n in ("q_summed", "a_summed", "t_done", "s_summed", "pv_summed", "o_summed"))
        xh_ready, qh_ready, shift_ready, prob_ready, ch_ready, normed = (
            sem(n) for n in ("xh_ready", "qh_ready", "shift_ready", "prob_ready", "ch_ready", "normed"))
        ql_ready, max_ready, rden_ready, cx_ready, y_ready, stats_ready, mv_ready, ve_ready, nmr_ready, const_dve = (
            sem(n) for n in ("ql_ready", "max_ready", "rden_ready", "cx_ready", "y_ready", "stats_ready",
                             "mv_ready", "ve_ready", "nmr_ready", "const_dve"))
        xl_ready, xb_ready, rstd_ready, scaled, y_done, cl_ready, const_pool, pool_zeroed = (
            sem(n) for n in ("xl_ready", "xb_ready", "rstd_ready", "scaled", "y_done", "cl_ready",
                             "const_pool", "pool_zeroed"))
        Z_DMAS, KB_DMAS, KSV_DMAS = 3 * HC, HC, 4

        def run(engine, slot):
            last_pair = (NG + LAG_STORE + PAIR - 1) // PAIR
            loop_from, loop_to = 2, NG // PAIR - 1
            for u in range(loop_from):
                for k in range(PAIR):
                    slot(Slot(u, k))
            with engine.Fori(loop_from, loop_to) as u:
                for k in range(PAIR):
                    slot(Slot(u, k))
            for u in range(loop_to, last_pair):
                for k in range(PAIR):
                    slot(Slot(u, k))

        block = ctx.enter_context(nc.Block())

        @block.sync
        def _(sp):
            def load_kb(b):
                i = b.k // NCH % 2
                all_at_least(sp, (a_summed, b.over(NCH, -1, NCH * QT)))
                src = kh_dram[b.over(NCH)]
                for j in range(HC):
                    sp.dma_start(kb[DK * j:DK * (j + 1), i, :, S2 * j:S2 * (j + 1)].bitcast(F32),
                                 src.rearrange("(c j d) k -> j d c k", j=HC, d=DK)[j]).then_inc(kb_in[i], 16)

            def load_ksv(b):
                i = b.k // NCH % 2
                all_at_least(sp, (s_summed, b.over(NCH, -1, NCH * HC)), (pv_summed, b.over(NCH, -1, NCH)))
                for part, src in enumerate((kh_dram, kl_dram, kh_dram)):
                    sp.dma_start(ks[DK * part:DK * (part + 1), i, :, :].bitcast(F32),
                                 src[b.over(NCH)].rearrange("(h d) k -> d h k", d=DK)).then_inc(ksv_in[i], 16)
                sp.dma_start(vb[0:S2, i, :], v_dram[b.over(NCH)]).then_inc(ksv_in[i], 16)

            def load_xt(n):
                all_at_least(sp, (xh_ready, n.over(1, -1)), (xl_ready, n.over(1, -1)))
                sp.dma_start(xt[:, n.k % 2, :], xt_dram[n.over(1)]).then_inc(xt_in[n.k % 2], 16)

            sp.dma_start(gamma[:], a["ln_gamma"].partition_broadcast(P)).then_inc(rows_in, 16)
            sp.dma_start(beta[:], a["ln_beta"].partition_broadcast(P)).then_inc(rows_in, 16)
            sp.dma_start(bo[:], a["bo"].partition_broadcast(P)).then_inc(rows_in, 16)
            for n in range(-LAG_LOAD_X):
                load_xt(Slot(0, n))
            sp.wait_ge(pool_zeroed, 1)
            load_kb(Slot(0, 0))

            def slot(g):
                if g.k % 2 == 0 and g.back(2).valid(NG):
                    c = g.back(2)
                    i = c.k // 2 % 2
                    all_at_least(sp, (qh_ready, c.over(1, 2)), (ql_ready, c.over(1, 2)),
                                 (s_summed, c.over(2, -1, HALF)))
                    for part, src in enumerate((qh, qh, ql)):
                        for j in range(HC):
                            sp.dma_start(z[DK * part:DK * (part + 1), i, j::HC, :].bitcast(F32),
                                         src[DK * j:DK * (j + 1), i, :, :].bitcast(F32)).then_inc(z_in[i], 16)
                if g.k % NCH == 1 and g.valid(NG):
                    load_ksv(g.back(1))
                if g.k % NCH == NCH - 1 and g.back(-1).valid(NG):
                    load_kb(g.back(-1))
                if g.back(LAG_LOAD_X).valid(NG):
                    load_xt(g.back(LAG_LOAD_X))
                m = g.back(LAG_NORM - 2)
                if m.valid(NM):
                    all_at_least(sp, (y_ready, m.over(1, -1)))
                    sp.dma_start(xn[:, m.k % 2, :], x_dram[m.over(1)]).then_inc(xn_in[m.k % 2], 16)
                m = g.back(LAG_STORE)
                if m.valid(NM):
                    all_at_least(sp, (y_done, m.over(1, 1)))
                    sp.dma_start(out_dram[m.over(1)], y[:, m.k % 4, :]).then_inc(stored[m.k % 4], 16)
            run(sp, slot)
            for i in range(4):
                sp.wait_ge(stored[i], 16 * (NM // 4))

        @block.tensor
        def _(pe):
            pe.wait_ge(const_pool, 2)
            pe.wait_ge(const_dve, 2)

            def project_q(g, kcs):
                i, c = g.k // NCH % 2, g.k % NCH
                if kcs[0] == 0:
                    if c == 0:
                        pe.wait_ge(xh_ready, g.over(NCH, 1, KC))
                        pe.wait_ge(xl_ready, g.over(NCH, 1, KC))
                    at_least(pe, ql_ready, g.over(1))
                for kc in kcs:
                    for n, (w, x) in enumerate(((wqh, xh), (wqh, xl), (wql, xh))):
                        last = nc.tensor.matmul(p_q[:], w[:, kc, P * c:P * (c + 1)], x[:, i, kc, :],
                                                start=(kc == 0 and n == 0), stop=(kc == KC - 1 and n == 2))
                if kcs[-1] == KC - 1:
                    last.then_inc(q_summed, 1)

            def rowmax_scores(g, t):
                if t == 0:
                    pe.wait_ge(qh_ready, g.over(1, 1))
                    if g.k % NCH == 0:
                        pe.wait_ge(kb_in[g.k // NCH % 2], g.over(PAIR, 1, 16 * KB_DMAS))
                if t < 2:
                    at_least(pe, max_ready, g.over(1, -1, QT) + t + 3)
                else:
                    pe.wait_ge(max_ready, g.over(1, 0, QT) + t - 1)
                s = g.back(LAG_SCORE - LAG_ROWMAX)
                if t == 1 and s.valid(NG):
                    pe.wait_ge(prob_ready, s.over(1, 0, HC) + HC - 1)
                nc.tensor.matmul(p_a[t % 2][:, 0:HC * S2], qh[:, g.k // 2 % 2, g.k % 2, P * t:P * (t + 1)],
                                 kb[:, g.k // NCH % 2, g.k % NCH, :], start=True, stop=True).then_inc(a_summed, 1)

            def turn_maxima(g):
                pe.wait_ge(max_ready, g.over(1, 2, QT))
                at_least(pe, shift_ready, g.over(2, 0, 2))
                for t in range(QT):
                    last = nc.tensor.transpose(p_t[0:HALF, P * t:P * (t + 1)], nm[:, g.k // 2 % 2, t, :], ident[:])
                last.then_inc(t_done, 1)

            def scores(g, j):
                i, s, h = g.k // 2 % 2, HC * (g.k % 2) + j, HC * (g.k % NCH) + j
                if j == 0:
                    pe.wait_ge(z_in[i], g.over(4, 1, 16 * Z_DMAS))
                    pe.wait_ge(shift_ready, g.over(1, 1))
                    if g.k % NCH == 0:
                        pe.wait_ge(ksv_in[g.k // NCH % 2], g.over(PAIR, 1, 16 * KSV_DMAS))
                at_least(pe, prob_ready, g.over(1, 0, HC) + j - 1)
                if j == 0:
                    newest = g.back(LAG_ROWMAX - LAG_SCORE + 1)
                    pe.wait_ge(max_ready, newest.over(1, 1, QT) if newest.valid(NG) else NG * QT)
                nc.tensor.matmul(p_s[j % 2][0:S2, :], ks[0:KR, g.k // NCH % 2, h, :], z[0:KR, i, s, :],
                                 start=True, stop=True).then_inc(s_summed, 1)

            def values(g):
                pe.wait_ge(prob_ready, g.over(1, 1, HC))
                at_least(pe, cx_ready, g.over(1))
                for j in range(HC):
                    h = HC * (g.k % NCH) + j
                    nc.tensor.matmul(p_v[DK * j:DK * (j + 1), :], vb[0:S2, g.k // NCH % 2, DK * h:DK * (h + 1)],
                                     prob[0:S2, j, :], start=True, stop=True)
                for j in range(HC):
                    last = nc.tensor.matmul(p_d[DK * j:DK * (j + 1), :], ones[0:S2, :], prob[0:S2, j, :],
                                            start=True, stop=True)
                last.then_inc(pv_summed, 1)

            def project_out(m, kc):
                i, t = m.k // QT % 2, m.k % QT
                if kc == 0:
                    if t == 0:
                        pe.wait_ge(ch_ready, m.over(QT, 1, KC))
                        pe.wait_ge(cl_ready, m.over(QT, 1, KC))
                    at_least(pe, y_ready, m.over(1))
                for n, (x, w) in enumerate(((ch, woh), (ch, wol), (cl, woh))):
                    last = nc.tensor.matmul(p_o[:], x[:, i, kc, P * t:P * (t + 1)], w[:, kc, :],
                                            start=(kc == 0 and n == 0), stop=(kc == KC - 1 and n == 2))
                if kc == KC - 1:
                    last.then_inc(o_summed, 1)

            def slot(g):
                q, r, s, v, o = g, g.back(LAG_ROWMAX), g.back(LAG_SCORE), g.back(LAG_PV), g.back(LAG_OUT)
                if v.valid(NG):
                    values(v)
                if g.k % 2 == 1 and g.back(3).valid(NG):
                    turn_maxima(g.back(3))
                if s.valid(NG):
                    scores(s, 0)
                    scores(s, 1)
                for half in range(2):
                    if q.valid(NG):
                        project_q(q, [2 * half, 2 * half + 1])
                    if s.valid(NG):
                        scores(s, 2 + half)
                    if r.valid(NG):
                        rowmax_scores(r, half)
                for t in range(QT):
                    if o.valid(NM):
                        project_out(o, t)
                    if r.valid(NG) and t < 2:
                        rowmax_scores(r, 2 + t)
            run(pe, slot)

        @block.scalar
        def _(act):
            def exp(g, j):
                act.wait_ge(s_summed, g.over(1, 0, HC) + j + 1)
                if j == 0:
                    at_least(act, pv_summed, g.over(1))
                nc.scalar.activation(prob[0:S2, j, :], p_s[j % 2][0:S2, :], ACT.Exp, scale=SCALE).then_inc(prob_ready, 1)

            def split_x_high(n):
                i = n.k // KC % 2
                act.wait_ge(xt_in[n.k % 2], n.over(2, 1, 16))
                if n.k % KC == 0:
                    at_least(act, q_summed, n.over(KC, -1, NCH))
                nc.scalar.copy(xh[:, i, n.k % KC, :], xt[:, n.k % 2, :]).then_inc(xh_ready, 1)

            def place_maxima(g, cc):
                i = g.k // 2 % 2
                if cc == 0:
                    act.wait_ge(t_done, g.over(2, 1))
                    at_least(act, s_summed, g.over(2, -1, HALF))
                nc.scalar.copy(z[QI:KR, i, HC * cc:HC * (cc + 1), :],
                               p_t[0:HALF, :].unsqueeze(1).broadcast_to([HALF, HC, S])).then_inc(shift_ready, 1)

            def q_high(g):
                i = g.k // 2 % 2
                act.wait_ge(q_summed, g.over(1, 1))
                at_least(act, a_summed, g.over(1, -3, QT))
                if g.k % 2 == 0:
                    at_least(act, z_in[i], g.over(4, 0, 16 * Z_DMAS))
                nc.scalar.activation(qh[:, i, g.k % 2, :], p_q[:], ACT.Identity,
                                     bias=bq_col[:, g.k % NCH:g.k % NCH + 1]).then_inc(qh_ready, 1)

            def ctx_high(g):
                i = g.k // NCH % 2
                act.wait_ge(cx_ready, g.over(1, 1))
                if g.k % NCH == 0:
                    at_least(act, o_summed, g.over(NCH, -1, QT))
                nc.scalar.copy(ch[:, i, g.k % NCH, :], cx[:, g.k % 2, :]).then_inc(ch_ready, 1)

            def normalize(m):
                i = m.k % 4
                act.wait_ge(nmr_ready, m.over(1, 1))
                nc.scalar.activation(y[:, i, :], y[:, i, :], ACT.Identity, bias=nmr[:, i, :],
                                     scale=rstd[:, i, :]).then_inc(normed, 1)

            for n in range(-LAG_SPLIT):
                split_x_high(Slot(0, n))

            def slot(g):
                s, v, m, n = g.back(LAG_SCORE), g.back(LAG_PV), g.back(LAG_NORM), g.back(LAG_SPLIT)
                turn = g.k % 2 == 1 and g.back(3).valid(NG)
                if s.valid(NG):
                    exp(s, 0)
                    exp(s, 1)
                if n.valid(NG):
                    split_x_high(n)
                if s.valid(NG):
                    exp(s, 2)
                if g.valid(NG):
                    q_high(g)
                if s.valid(NG):
                    exp(s, 3)
                if turn:
                    place_maxima(g.back(3), 0)
                if v.valid(NG):
                    ctx_high(v)
                if m.valid(NM):
                    normalize(m)
                if turn:
                    place_maxima(g.back(3), 1)
            run(act, slot)

        @block.vector
        def _(dve):
            nc.vector.memset(minus_half[:], -0.5).then_inc(const_dve, 1)
            dve.wait_ge(const_pool, 2)
            for i in range(2):
                for hf in range(2):
                    last = nc.vector.tensor_copy(ks[QI:KR, i, HALF * hf:HALF * (hf + 1), :],
                                                 ident[0:HALF, 0:HALF].unsqueeze(2).broadcast_to([HALF, HALF, S2]))
            last.then_inc(const_dve, 1)

            def add_residual(m):
                i = m.k % 4
                dve.wait_ge(o_summed, m.over(1, 1))
                dve.wait_ge(xb_ready, m.over(1, 1))
                at_least(dve, stored[i], m.over(4, 0, 16))
                nc.vector.tensor_tensor(y[:, i, :], p_o[:], xn[:, m.k % 2, :], ALU.add).then_inc(y_ready, 1)
                dve.wait_ge(y_ready, m.over(1, 1))
                nc.vector.bn_stats(stats[:, i, :], y[:, i, :]).then_inc(stats_ready, 1)

            def invert_sums(g):
                dve.wait_ge(pv_summed, g.over(1, 1))
                nc.vector.reciprocal(rden[:], p_d[:]).then_inc(rden_ready, 1)

            def variance(m):
                i = m.k % 4
                nc.vector.bn_aggr(mv[:, i, :], stats[:, i, :]).then_inc(mv_ready, 1)
                dve.wait_ge(mv_ready, m.over(1, 1))
                nc.vector.tensor_scalar(ve[:, i, :], mv[:, i, 1:2], EPS, None, ALU.add).then_inc(ve_ready, 1)

            def divide(g):
                i = g.k % 2
                dve.wait_ge(rden_ready, g.over(1, 1))
                at_least(dve, ch_ready, g.over(1, -1))
                at_least(dve, cl_ready, g.over(1, -1))
                nc.vector.tensor_tensor(cx[:, i, :], p_v[:], rden[:], ALU.mult).then_inc(cx_ready, 1)

            def mean_over_std(m):
                i = m.k % 4
                dve.wait_ge(rstd_ready, m.over(1, 1))
                nc.vector.scalar_tensor_tensor(out=nmr[:, i, :], in0=mv[:, i, 0:1], scalar=-1.0, in1=rstd[:, i, :],
                                               op0=ALU.mult, op1=ALU.mult).then_inc(nmr_ready, 1)

            def q_low(g):
                i = g.k // 2 % 2
                dve.wait_ge(qh_ready, g.over(1, 1))
                if g.k % 2 == 0:
                    at_least(dve, z_in[i], g.over(4, 0, 16 * Z_DMAS))
                nc.vector.scalar_tensor_tensor(
                    out=ql[:, i, g.k % 2, :], in0=p_q[:], scalar=bq_col[:, g.k % NCH:g.k % NCH + 1],
                    in1=qh[:, i, g.k % 2, :].bitcast(F32), op0=ALU.add, op1=ALU.subtract).then_inc(ql_ready, 1)

            def row_maxima(g, t):
                i = g.k // 2 % 2
                dve.wait_ge(a_summed, g.over(1, 0, QT) + t + 1)
                if t == 0 and g.k % 2 == 0:
                    at_least(dve, t_done, g.over(2, -1))
                nc.vector.tensor_reduce(nm[:, i, t, HC * (g.k % 2):HC * (g.k % 2 + 1)],
                                        p_a[t % 2][:, 0:HC * S2].rearrange("p (h k) -> p h k", k=S2),
                                        AX_X, ALU.max, negate=True).then_inc(max_ready, 1)

            def slot(g):
                r, v, m = g.back(LAG_ROWMAX), g.back(LAG_PV), g.back(LAG_NORM)
                if m.valid(NM):
                    add_residual(m)
                    dve.wait_ge(stats_ready, m.over(1, 1))
                if v.valid(NG):
                    invert_sums(v)
                if r.valid(NG):
                    row_maxima(r, 0)
                if v.valid(NG):
                    divide(v)
                if m.valid(NM):
                    variance(m)
                if r.valid(NG):
                    row_maxima(r, 1)
                if g.valid(NG):
                    q_low(g)
                if r.valid(NG):
                    row_maxima(r, 2)
                    row_maxima(r, 3)
                if m.valid(NM):
                    mean_over_std(m)
            run(dve, slot)

        @block.gpsimd
        def _(pool):
            nc.gpsimd.memset(ident[:], 0.0).then_inc(const_pool, 1)
            nc.gpsimd.memset(kb[:].bitcast(F32), 0.0).then_inc(pool_zeroed, 1)
            nc.gpsimd.memset(ones[:], 1.0)
            pool.wait_ge(const_pool, 1)
            pool.wait_ge(pool_zeroed, 1)
            nc.gpsimd.affine_select(out=ident[:], in_=ident[:], compare_op=ALU.not_equal, fill=1.0, base=0,
                                    pattern=[[-1, P]], channel_multiplier=1).then_inc(const_pool, 1)

            def split_x_low(n):
                i = n.k // KC % 2
                pool.wait_ge(xh_ready, n.over(1, 1))
                nc.gpsimd.tensor_tensor(xl[:, i, n.k % KC, :], xt[:, n.k % 2, :],
                                        xh[:, i, n.k % KC, :].bitcast(F32), ALU.subtract).then_inc(xl_ready, 1)

            def inverse_std(m):
                i = m.k % 4
                pool.wait_ge(ve_ready, m.over(1, 1))
                nc.gpsimd.tensor_tensor(rstd[:, i, :], ve[:, i, :], minus_half[:], ALU.pow).then_inc(rstd_ready, 1)

            def scale_shift(m):
                i = m.k % 4
                pool.wait_ge(normed, m.over(1, 1))
                nc.gpsimd.tensor_tensor(y[:, i, :], y[:, i, :], gamma[:], ALU.mult).then_inc(scaled, 1)
                pool.wait_ge(scaled, m.over(1, 1))
                nc.gpsimd.tensor_tensor(y[:, i, :], y[:, i, :], beta[:], ALU.add).then_inc(y_done, 1)

            def ctx_low(g):
                i = g.k // NCH % 2
                pool.wait_ge(ch_ready, g.over(1, 1))
                nc.gpsimd.tensor_tensor(cl[:, i, g.k % NCH, :], cx[:, g.k % 2, :],
                                        ch[:, i, g.k % NCH, :].bitcast(F32), ALU.subtract).then_inc(cl_ready, 1)

            def add_bo(m):
                pool.wait_ge(xn_in[m.k % 2], m.over(2, 1, 16))
                nc.gpsimd.tensor_tensor(xn[:, m.k % 2, :], xn[:, m.k % 2, :], bo[:], ALU.add).then_inc(xb_ready, 1)

            pool.wait_ge(rows_in, 48)
            pool.wait_ge(const_dve, 1)
            for n in range(-LAG_SPLIT):
                split_x_low(Slot(0, n))

            def slot(g):
                v, m, n, b = g.back(LAG_PV), g.back(LAG_NORM), g.back(LAG_SPLIT), g.back(LAG_NORM - 1)
                if g.back(LAG_SCALE).valid(NM):
                    scale_shift(g.back(LAG_SCALE))
                if n.valid(NG):
                    split_x_low(n)
                if b.valid(NM):
                    add_bo(b)
                if m.valid(NM):
                    inverse_std(m)
                if v.valid(NG):
                    ctx_low(v)
            run(pool, slot)


def xattn(nc, a, out):
    B, S, _ = a["x"].shape
    S2 = a["ctx_t"].shape[1] // B
    kh_dram = nc.dram_tensor("k_high", (B, D, S2), F32, kind="Internal").ap()
    kl_dram = nc.dram_tensor("k_low", (B, D, S2), F32, kind="Internal").ap()
    v_dram = nc.dram_tensor("v_all", (B, S2, D), F32, kind="Internal").ap()
    with ExitStack() as ctx:
        keep = {n: ctx.enter_context(nc.sbuf_tensor(n, [P, KC, D], F32R)) for n in ("wqh", "wql", "woh", "wol")}
        keep["bq_col"] = ctx.enter_context(nc.sbuf_tensor("bq_col", [P, KC], F32))
        bq_in = ctx.enter_context(nc.semaphore("bq_in"))
        with nc.Block() as block:
            @block.sync
            def _(sp):
                sp.dma_start(keep["bq_col"][:], a["bq"]).then_inc(bq_in, 16)
                sp.wait_ge(bq_in, 16)
        project_context(nc, a, keep, kh_dram, kl_dram, v_dram.rearrange("b k d -> (b k) d"), B, S2)
        attend(nc, a, keep, kh_dram, kl_dram, v_dram, out, B, S, S2)


def kernel(**inputs):
    import numpy as np
    import concourse.bacc as bacc
    from concourse.bass_utils import run_bass_kernel_spmd

    x = np.ascontiguousarray(inputs["x"])
    context = np.asarray(inputs["ctx_1024"])
    w = {n: np.asarray(inputs[f"L0_xattn_{n}"])
         for n in ("Wq", "bq", "Wk", "bk", "Wv", "bv", "Wo", "bo", "ln_gamma", "ln_beta")}
    arrays = {"x": x, "x_t": np.ascontiguousarray(x.transpose(0, 2, 1)),
              "ctx_t": np.ascontiguousarray(context.reshape(-1, D).T)}
    for n, v in w.items():
        arrays[n] = np.ascontiguousarray(v.reshape(KC, P).T if n in ("bq", "bk") else v)
    nc = bacc.Bacc("TRN2", target_bir_lowering=False, num_devices=1)
    a = {n: nc.dram_tensor(f"in_{n}", v.shape, mybir.dt.from_np(v.dtype), kind="ExternalInput").ap()
         for n, v in arrays.items()}
    out = nc.dram_tensor("out_0_dram", x.shape, F32, kind="ExternalOutput").ap()
    xattn(nc, a, out)
    r = run_bass_kernel_spmd(nc, [{f"in_{n}": v for n, v in arrays.items()}], core_ids=[0])
    return r.results[0]["out_0_dram"]
```

```python
from contextlib import ExitStack

import concourse.bass as bass
from concourse import mybir

F32 = mybir.dt.float32
F32R = mybir.dt.float32r
ALU = mybir.AluOpType
ACT = mybir.ActivationFunctionType
AX_X = mybir.AxisListType.X

P = 128
D = 512
KC = D // P
DK = 32
HC = P // DK
NCH = D // P
HALF = 2 * HC
PAIR = 2 * NCH
EPS = 1e-5

LAG_SPLIT = -4
LAG_LOAD_X = -5
LAG_ROWMAX = 1
LAG_PV = 5
LAG_SCORE = 4
LAG_OUT = 9
LAG_NORM = 10
LAG_SCALE = 11
LAG_STORE = 12


class Slot:

    def __init__(self, u, k):
        self.u, self.k = u, k

    def back(self, lag):
        return Slot(self.u, self.k - lag)

    def over(self, d, plus=0, times=1):
        return self.u * (PAIR // d * times) + (self.k // d + plus) * times

    def valid(self, n):
        return not isinstance(self.u, int) or 0 <= PAIR * self.u + self.k < n

    def is_first(self):
        return isinstance(self.u, int) and PAIR * self.u + self.k == 0


def at_least(engine, sem, value):
    if not isinstance(value, int) or value > 0:
        engine.wait_ge(sem, value)


def all_at_least(engine, *waits):
    for _, value in waits:
        if not isinstance(value, int):
            engine.compute_val(value)
    for sem, value in waits:
        at_least(engine, sem, value)


def project_context(nc, a, keep, kh_dram, kl_dram, v_dram, B, S2):
    NK = B * S2
    NT = 3
    cuts = [0] + [(NK * (i + 1) // NT + 1) // 2 * 2 for i in range(NT - 1)] + [NK]
    tiles_k = [(c, cuts[i], cuts[i + 1]) for c in range(KC) for i in range(NT)]
    tiles_v = [(r, min(P, NK - r)) for r in range(0, NK, P)]
    PK = 2 * NT
    CX = 3
    xt, xh, xl, y = (keep[n] for n in ("xt", "xh", "xl", "y"))
    xt_in, xh_ready, xl_ready, v_stored, const_pool = (
        keep[n] for n in ("xt_in", "xh_ready", "xl_ready", "v_stored", "const_pool"))
    with ExitStack() as ctx:
        def sb(name, shape, dt):
            return ctx.enter_context(nc.sbuf_tensor(name, shape, dt))

        def sem(name):
            return ctx.enter_context(nc.semaphore(name))

        cx = sb("cx", [P, CX, NK], F32)
        cxh, cxl = sb("cxh", [P, KC, NK], F32R), sb("cxl", [P, KC, NK], F32R)
        w_raw = [sb(f"w_raw{i}", [P, KC, D], F32) for i in range(2)]
        wkh, wkl = sb("wkh", [P, KC, D], F32R), sb("wkl", [P, KC, D], F32R)
        wvh, wvl = sb("wvh", [P, KC, D], F32R), sb("wvl", [P, KC, D], F32R)
        kth, ktl = sb("kth", [P, 2, NK], F32R), sb("ktl", [P, 2, NK], F32R)
        bv_row = sb("bv_row", [P, D], F32)
        bk_col = sb("bk_col", [P, KC], F32)
        pk = [ctx.enter_context(nc.psum_tensor(f"pk{i}", [P, D], F32)) for i in range(PK)]
        pv = [ctx.enter_context(nc.psum_tensor(f"pvv{i}", [P, D], F32)) for i in range(2)]

        chunk_in = [sem(f"chunk_in{i}") for i in range(KC)]
        biases_in, wv_in, wq_in, wo_in = (sem(n) for n in ("biases_in", "wv_in", "wq_in", "wo_in"))
        kv_high, kv_low, qo_high, qo_low = (sem(n) for n in ("kv_high", "kv_low", "qo_high", "qo_low"))
        k_summed, k_high_out, k_low_out = sem("k_summed"), sem("k_high_out"), sem("k_low_out")
        v_summed, v_out = sem("v_summed"), sem("v_out")
        k_stored = [sem(f"k_stored{i}") for i in range(2)]
        first = [part for kc in range(KC) for part in ((cx[:, kc % CX, :], cxh[:, kc, :], cxl[:, kc, :]),
                                                       (w_raw[0][:, kc, :], wkh[:, kc, :], wkl[:, kc, :]))]
        first += [(w_raw[1][:, kc, :], wvh[:, kc, :], wvl[:, kc, :]) for kc in range(KC)]
        second = [(w_raw[0][:, kc, :], keep["wqh"][:, kc, :], keep["wql"][:, kc, :]) for kc in range(KC)]
        second += [(w_raw[1][:, kc, :], keep["woh"][:, kc, :], keep["wol"][:, kc, :]) for kc in range(KC)]

        with nc.Block() as block:
            @block.sync
            def _(sp):
                def load_xt(n):
                    if n >= 2:
                        sp.wait_ge(xh_ready, n - 1)
                        sp.wait_ge(xl_ready, n - 1)
                    sp.dma_start(xt[:, n % 2, :], a["x_t"][0, P * n:P * (n + 1), :]).then_inc(xt_in[n % 2], 16)

                def by_chunk(w):
                    return w.rearrange("(c p) n -> p c n", p=P)

                for kc in range(KC):
                    if kc >= CX:
                        sp.wait_ge(kv_high, 2 * (kc - CX) + 1)
                        sp.wait_ge(kv_low, 2 * (kc - CX) + 1)
                    sp.dma_start(cx[:, kc % CX, :], a["ctx_t"][P * kc:P * (kc + 1), :]).then_inc(chunk_in[kc], 16)
                    sp.dma_start(w_raw[0][:, kc, :], a["Wk"][P * kc:P * (kc + 1), :]).then_inc(chunk_in[kc], 16)
                sp.dma_start(bk_col[:], a["bk"]).then_inc(biases_in, 16)
                sp.dma_start(bv_row[:], a["bv"].partition_broadcast(P)).then_inc(biases_in, 16)
                sp.dma_start(w_raw[1][:], by_chunk(a["Wv"])).then_inc(wv_in, 16)
                load_xt(0)
                load_xt(1)
                sp.wait_ge(kv_high, 2 * KC)
                sp.wait_ge(kv_low, 2 * KC)
                sp.dma_start(w_raw[0][:], by_chunk(a["Wq"])).then_inc(wq_in, 16)

                for c in range(KC):
                    sp.wait_ge(k_high_out, NT * (c + 1))
                    sp.wait_ge(k_low_out, NT * (c + 1))
                    for t, dst in ((kth, kh_dram), (ktl, kl_dram)):
                        sp.dma_start(dst[P * c:P * (c + 1), :], t[:, c % 2, :].bitcast(F32)).then_inc(k_stored[c % 2], 16)
                    if c == 1:
                        load_xt(2)
                        load_xt(3)
                        sp.wait_ge(kv_high, 3 * KC)
                        sp.wait_ge(kv_low, 3 * KC)
                        sp.dma_start(w_raw[1][:], by_chunk(a["Wo"])).then_inc(wo_in, 16)
                for i in range(2):
                    sp.wait_ge(k_stored[i], 16 * KC)
                sp.wait_ge(keep["kb0_zeroed"], 1)
                src = kh_dram.rearrange("(c j d) (b k) -> b j d c k", j=HC, d=DK, k=S2)[0]
                for j in range(HC):
                    sp.dma_start(keep["kb0"][DK * j:DK * (j + 1), :, S2 * j:S2 * (j + 1)].bitcast(F32),
                                 src[j]).then_inc(keep["kb_in"][0], 16)
                for i, (r, n) in enumerate(tiles_v):
                    sp.wait_ge(v_out, i + 1)
                    sp.dma_start(v_dram[r:r + n, :], y[0:n, i % 4, :]).then_inc(v_stored[i % 4], 16)

            @block.scalar
            def _(act):
                def high(part, signal):
                    raw, hi, _ = part
                    nc.scalar.copy(hi, raw).then_inc(signal, 1)

                def k_high(i):
                    c, lo, hi = tiles_k[i]
                    act.wait_ge(k_summed, i + 1)
                    if c >= 2:
                        act.wait_ge(k_stored[c % 2], 32)
                    nc.scalar.activation(kth[:, c % 2, lo:hi], pk[i % PK][:, 0:hi - lo], ACT.Identity,
                                         bias=bk_col[:, c:c + 1]).then_inc(k_high_out, 1)

                def x_high(n):
                    act.wait_ge(xt_in[n % 2], 16 * (n // 2 + 1))
                    nc.scalar.copy(xh[:, 0, n, :], xt[:, n % 2, :]).then_inc(xh_ready, 1)

                for kc in range(KC):
                    act.wait_ge(chunk_in[kc], 32)
                    high(first[2 * kc], kv_high)
                    high(first[2 * kc + 1], kv_high)
                act.wait_ge(biases_in, 32)
                for i in range(PK):
                    k_high(i)
                act.wait_ge(wv_in, 16)
                for kc in range(KC):
                    high(first[2 * KC + kc], kv_high)
                x_high(0)
                x_high(1)
                act.wait_ge(wq_in, 16)
                for i in range(PK, 2 * PK):
                    k_high(i)
                    if i - PK < KC:
                        high(second[i - PK], qo_high)
                x_high(2)
                x_high(3)
                act.wait_ge(wo_in, 16)
                for kc in range(KC):
                    high(second[KC + kc], qo_high)

            @block.vector
            def _(dve):
                def low(i):
                    raw, hi, lo = first[i]
                    dve.wait_ge(kv_high, i + 1)
                    nc.vector.tensor_tensor(lo, raw, hi.bitcast(F32), ALU.subtract).then_inc(kv_low, 1)

                def k_low(i):
                    c, lo, hi = tiles_k[i]
                    dve.wait_ge(k_high_out, i + 1)
                    if c >= 2:
                        dve.wait_ge(k_stored[c % 2], 32)
                    nc.vector.scalar_tensor_tensor(
                        out=ktl[:, c % 2, lo:hi], in0=pk[i % PK][:, 0:hi - lo], scalar=bk_col[:, c:c + 1],
                        in1=kth[:, c % 2, lo:hi].bitcast(F32), op0=ALU.add, op1=ALU.subtract).then_inc(k_low_out, 1)

                for i in range(2 * KC):
                    low(i)
                dve.wait_ge(biases_in, 32)
                for i in range(PK):
                    k_low(i)
                for kc in range(KC):
                    low(2 * KC + kc)
                for i in range(PK, 2 * PK):
                    k_low(i)
                for i, (r, n) in enumerate(tiles_v):
                    dve.wait_ge(v_summed, i + 1)
                    if i >= 4:
                        dve.wait_ge(v_stored[i % 4], 16 * (i // 4))
                    nc.vector.tensor_tensor(y[0:n, i % 4, :], pv[i % 2][0:n, :], bv_row[0:n, :],
                                            ALU.add).then_inc(v_out, 1)

            @block.gpsimd
            def _(pool):
                ident = keep["ident"]
                nc.gpsimd.memset(ident[:], 0.0).then_inc(const_pool, 1)
                nc.gpsimd.memset(keep["kb0"][:].bitcast(F32), 0.0).then_inc(keep["kb0_zeroed"], 1)
                nc.gpsimd.memset(keep["ones"][:], 1.0)
                nc.gpsimd.memset(keep["minus_half"][:], -0.5)
                pool.wait_ge(const_pool, 1)
                nc.gpsimd.affine_select(out=ident[:], in_=ident[:], compare_op=ALU.not_equal, fill=1.0, base=0,
                                        pattern=[[-1, P]], channel_multiplier=1).then_inc(const_pool, 1)

                def x_low(n):
                    pool.wait_ge(xh_ready, n + 1)
                    nc.gpsimd.tensor_tensor(xl[:, 0, n, :], xt[:, n % 2, :], xh[:, 0, n, :].bitcast(F32),
                                            ALU.subtract).then_inc(xl_ready, 1)

                def qo_lows(base):
                    for i in range(base, base + KC):
                        raw, hi, lo = second[i]
                        pool.wait_ge(qo_high, i + 1)
                        nc.gpsimd.tensor_tensor(lo, raw, hi.bitcast(F32), ALU.subtract).then_inc(qo_low, 1)
                x_low(0)
                x_low(1)
                qo_lows(0)
                x_low(2)
                x_low(3)
                qo_lows(KC)

            @block.tensor
            def _(pe):
                def k_products(i, kc):
                    c, lo, hi = tiles_k[i]
                    for n, (w, x) in enumerate(((wkh, cxh), (wkh, cxl), (wkl, cxh))):
                        last = nc.tensor.matmul(pk[i % PK][:, 0:hi - lo], w[:, kc, P * c:P * (c + 1)], x[:, kc, lo:hi],
                                                start=(kc == 0 and n == 0), stop=(kc == KC - 1 and n == 2))
                    if kc == KC - 1:
                        last.then_inc(k_summed, 1)

                for kc in range(KC):
                    pe.wait_ge(kv_low, 2 * (kc + 1))
                    for i in range(PK):
                        k_products(i, kc)
                for i in range(PK, 2 * PK):
                    pe.wait_ge(k_low_out, i - PK + 1)
                    for kc in range(KC):
                        k_products(i, kc)
                pe.wait_ge(kv_low, 3 * KC)
                for i, (r, m) in enumerate(tiles_v):
                    if i >= 2:
                        pe.wait_ge(v_out, i - 1)
                    for kc in range(KC):
                        for n, (x, w) in enumerate(((cxh, wvh), (cxh, wvl), (cxl, wvh))):
                            last = nc.tensor.matmul(pv[i % 2][0:m, :], x[:, kc, r:r + m], w[:, kc, :],
                                                    start=(kc == 0 and n == 0), stop=(kc == KC - 1 and n == 2))
                    last.then_inc(v_summed, 1)


def attend(nc, a, keep, kh_dram, kl_dram, v_dram, out, B, S, S2):
    NG = B * NCH
    QT = S // P
    NM = B * QT
    NS = NM - QT
    assert QT == NCH and B % 2 == 0
    SCALE = float(DK) ** -0.5
    QI = 3 * DK
    KR = QI + HALF

    wqh, wql, woh, wol, bq_col = (keep[n] for n in ("wqh", "wql", "woh", "wol", "bq_col"))
    xt, xh, xl, y, ident, ones, minus_half = (
        keep[n] for n in ("xt", "xh", "xl", "y", "ident", "ones", "minus_half"))
    xt_in, xh_ready, xl_ready = (keep[n] for n in ("xt_in", "xh_ready", "xl_ready"))
    xt_dram = a["x_t"].rearrange("b (c p) s -> (b c) p s", p=P)
    x_dram = a["x"].rearrange("b (t p) d -> (b t) p d", p=P)
    out_dram = out.rearrange("b (t p) d -> (b t) p d", p=P)
    with ExitStack() as ctx:
        def sb(name, shape, dt):
            return ctx.enter_context(nc.sbuf_tensor(name, shape, dt))

        def psum(name):
            return ctx.enter_context(nc.psum_tensor(name, [P, 512], F32))

        def sem(name):
            return ctx.enter_context(nc.semaphore(name))

        qh, ql = (sb(n, [P, 2, 2, S], F32R) for n in ("qh", "ql"))
        z = sb("z", [P, 2, HALF, S], F32R)
        ks = sb("ks", [P, 2, NCH * HC, S2], F32R)
        kb = [keep["kb0"], sb("kb1", [P, NCH, HC * S2], F32R)]
        vb = sb("vb", [P, 2, D], F32)
        nm = sb("nm", [P, 2, QT, HALF], F32)
        prob = sb("prob", [P, HC, S], F32)
        rden = sb("rden", [P, S], F32)
        cx = sb("cxt", [P, 2, S], F32)
        ch, cl = (sb(n, [P, 2, KC, S], F32R) for n in ("ch", "cl"))
        xn = sb("xn", [P, 2, D], F32)
        xn_last = sb("xn_last", [P, D], F32)
        stats = sb("stats", [P, 4, 6], F32)
        mv = sb("mv", [P, 4, 2], F32)
        ve, rstd, nmr = (sb(n, [P, 4, 1], F32) for n in ("ve", "rstd", "nmr"))
        gamma, beta, bo = (sb(n, [P, D], F32) for n in ("gamma_row", "beta_row", "bo_row"))
        p_q, p_t, p_v, p_d, p_o = (psum(n) for n in ("p_q", "p_t", "p_v", "p_d", "p_o"))
        p_s = [psum(f"p_s{i}") for i in range(2)]
        p_a = [psum("p_a"), p_s[0]]

        xn_in = [sem(f"xn_in{i}") for i in range(2)]
        kb_in = keep["kb_in"]
        ksv_in = [sem(f"ksv_in{i}") for i in range(2)]
        z_in = [sem(f"z_in{i}") for i in range(2)]
        stored = [sem(f"stored{i}") for i in range(4)]
        rows_in = sem("rows_in")
        x_last_in = [sem(f"x_last_in{t}") for t in range(QT)]
        q_summed, a_summed, t_done, s_summed, pv_summed, o_summed = (
            sem(n) for n in ("q_summed", "a_summed", "t_done", "s_summed", "pv_summed", "o_summed"))
        qh_ready, shift_ready, prob_ready, ch_ready, normed = (
            sem(n) for n in ("qh_ready", "shift_ready", "prob_ready", "ch_ready", "normed"))
        ql_ready, max_ready, rden_ready, cx_ready, y_ready, stats_ready, mv_ready, ve_ready, nmr_ready, const_dve, y_last_scaled, y_last_done = (
            sem(n) for n in ("ql_ready", "max_ready", "rden_ready", "cx_ready", "y_ready", "stats_ready",
                             "mv_ready", "ve_ready", "nmr_ready", "const_dve", "y_last_scaled", "y_last_done"))
        xb_ready, rstd_ready, scaled, y_done, cl_ready, kb1_zeroed, xb_last_ready = (
            sem(n) for n in ("xb_ready", "rstd_ready", "scaled", "y_done", "cl_ready", "kb1_zeroed", "xb_last_ready"))
        Z_DMAS, KB_DMAS, KSV_DMAS = 3 * HC, HC, 4
        V_TILES = -(-B * S2 // P)

        last_banks = [(p_q, ql_ready, NG), (p_a[0], max_ready, NG * QT), (p_t, shift_ready, NG),
                      (p_s[0], prob_ready, NG * HC)]
        x_last = [xt[:, 0, :], xt[:, 1, :], vb[:, B % 2, :], xn_last[:]]
        ON_POOL = 2

        def rows(m):
            if isinstance(m.u, int) and PAIR * m.u + m.k >= NS:
                return x_last[m.k % QT]
            return y[:, m.k % 4, :]

        def last_batch_chunk(g, lag):
            if isinstance(g.u, int) and 0 <= PAIR * g.u + g.k - lag - (NG - NCH) < NCH:
                return PAIR * g.u + g.k - lag - (NG - NCH)
            return None

        def run(engine, slot):
            loop_from, loop_to = 2, NG // PAIR - 1
            for u in range(loop_from):
                for k in range(PAIR):
                    slot(Slot(u, k))
            with engine.Fori(loop_from, loop_to) as u:
                for k in range(PAIR):
                    slot(Slot(u, k))
            for k in range(PAIR * loop_to, NG + LAG_PV):
                slot(Slot(k // PAIR, k % PAIR))

        kh_dram, kl_dram = (k.rearrange("d (b k) -> b d k", k=S2) for k in (kh_dram, kl_dram))

        block = ctx.enter_context(nc.Block())

        @block.sync
        def _(sp):
            def load_kb(b):
                i = b.k // NCH % 2
                all_at_least(sp, (a_summed, b.over(NCH, -1, NCH * QT)))
                src = kh_dram[b.over(NCH)]
                for j in range(HC):
                    sp.dma_start(kb[i][DK * j:DK * (j + 1), :, S2 * j:S2 * (j + 1)].bitcast(F32),
                                 src.rearrange("(c j d) k -> j d c k", j=HC, d=DK)[j]).then_inc(kb_in[i], 16)

            def load_ksv(b):
                i = b.k // NCH % 2
                all_at_least(sp, (s_summed, b.over(NCH, -1, NCH * HC)), (pv_summed, b.over(NCH, -1, NCH)))
                for part, src in enumerate((kh_dram, kl_dram, kh_dram)):
                    sp.dma_start(ks[DK * part:DK * (part + 1), i, :, :].bitcast(F32),
                                 src[b.over(NCH)].rearrange("(h d) k -> d h k", d=DK)).then_inc(ksv_in[i], 16)
                sp.dma_start(vb[0:S2, i, :], v_dram[b.over(NCH)]).then_inc(ksv_in[i], 16)

            def load_xt(n):
                all_at_least(sp, (xh_ready, n.over(1, -1)), (xl_ready, n.over(1, -1)))
                sp.dma_start(xt[:, n.k % 2, :], xt_dram[n.over(1)]).then_inc(xt_in[n.k % 2], 16)

            for n in range(KC, -LAG_LOAD_X):
                load_xt(Slot(0, n))
            for i in range(4):
                sp.wait_ge(keep["v_stored"][i], 16 * ((V_TILES + 3 - i) // 4))
            sp.dma_start(gamma[:], a["ln_gamma"].partition_broadcast(P)).then_inc(rows_in, 16)
            sp.dma_start(beta[:], a["ln_beta"].partition_broadcast(P)).then_inc(rows_in, 16)
            sp.dma_start(bo[:], a["bo"].partition_broadcast(P)).then_inc(rows_in, 16)

            def slot(g):
                if g.k % 2 == 0 and g.back(2).valid(NG):
                    c = g.back(2)
                    i = c.k // 2 % 2
                    all_at_least(sp, (qh_ready, c.over(1, 2)), (ql_ready, c.over(1, 2)),
                                 (s_summed, c.over(2, -1, HALF)))
                    for part, src in enumerate((qh, qh, ql)):
                        for j in range(HC):
                            sp.dma_start(z[DK * part:DK * (part + 1), i, j::HC, :].bitcast(F32),
                                         src[DK * j:DK * (j + 1), i, :, :].bitcast(F32)).then_inc(z_in[i], 16)
                if g.k % NCH == 1 and g.valid(NG):
                    load_ksv(g.back(1))
                if g.k % NCH == NCH - 1 and g.back(-1).valid(NG):
                    if g.back(NCH - 1).is_first():
                        sp.wait_ge(kb1_zeroed, 1)
                    load_kb(g.back(-1))
                if g.back(LAG_LOAD_X).valid(NG):
                    load_xt(g.back(LAG_LOAD_X))
                m = g.back(LAG_NORM - 2)
                if m.valid(NS):
                    all_at_least(sp, (y_ready, m.over(1, -1)))
                    sp.dma_start(xn[:, m.k % 2, :], x_dram[m.over(1)]).then_inc(xn_in[m.k % 2], 16)
                if last_batch_chunk(g, 1) == NCH - 1:
                    for t in range(QT):
                        if t == 0:
                            sp.wait_ge(xh_ready, NG)
                            sp.wait_ge(xl_ready, NG)
                        if t == 2:
                            sp.wait_ge(pv_summed, NG - NCH)
                        sp.dma_start(x_last[t], x_dram[NS + t]).then_inc(x_last_in[t], 16)
                if g.back(LAG_STORE).valid(NS):
                    store(g.back(LAG_STORE))

            def store(m):
                all_at_least(sp, (y_done, m.over(1, 1)))
                sp.dma_start(out_dram[m.over(1)], y[:, m.k % 4, :]).then_inc(stored[m.k % 4], 16)
            run(sp, slot)

            for m in range(NG + LAG_PV - LAG_STORE, NS):
                store(Slot(0, m))
            for t in (0, 2, 1, 3):
                if t < ON_POOL:
                    sp.wait_ge(y_done, NS + t + 1)
                else:
                    sp.wait_ge(y_last_done, t - ON_POOL + 1)
                sp.dma_start(out_dram[NS + t], x_last[t]).then_inc(stored[t], 16)
            for i in range(4):
                sp.wait_ge(stored[i], 16 * (NM // 4))

        @block.tensor
        def _(pe):
            def project_q(g, kc):
                i, c = g.k // NCH % 2, g.k % NCH
                if kc == 0:
                    if c == 0:
                        pe.wait_ge(xh_ready, g.over(NCH, 1, KC))
                        pe.wait_ge(xl_ready, g.over(NCH, 1, KC))
                    at_least(pe, ql_ready, g.over(1))
                for n, (w, x) in enumerate(((wqh, xh), (wqh, xl), (wql, xh))):
                    last = nc.tensor.matmul(p_q[:], w[:, kc, P * c:P * (c + 1)], x[:, i, kc, :],
                                            start=(kc == 0 and n == 0), stop=(kc == KC - 1 and n == 2))
                if kc == KC - 1:
                    last.then_inc(q_summed, 1)

            def rowmax_scores(g, t):
                if t == 0:
                    pe.wait_ge(qh_ready, g.over(1, 1))
                    if g.k % NCH == 0:
                        pe.wait_ge(kb_in[g.k // NCH % 2], g.over(PAIR, 1, 16 * KB_DMAS))
                if t < 2:
                    at_least(pe, max_ready, g.over(1, -1, QT) + t + 3)
                else:
                    pe.wait_ge(max_ready, g.over(1, 0, QT) + t - 1)
                s = g.back(LAG_SCORE - LAG_ROWMAX)
                if t == 1 and s.valid(NG):
                    pe.wait_ge(prob_ready, s.over(1, 0, HC) + HC - 1)
                nc.tensor.matmul(p_a[t % 2][:, 0:HC * S2], qh[:, g.k // 2 % 2, g.k % 2, P * t:P * (t + 1)],
                                 kb[g.k // NCH % 2][:, g.k % NCH, :], start=True, stop=True).then_inc(a_summed, 1)

            def turn_maxima(g):
                pe.wait_ge(max_ready, g.over(1, 2, QT))
                at_least(pe, shift_ready, g.over(2, 0, 2))
                for t in range(QT):
                    last = nc.tensor.transpose(p_t[0:HALF, P * t:P * (t + 1)], nm[:, g.k // 2 % 2, t, :], ident[:])
                last.then_inc(t_done, 1)

            def scores(g, j):
                i, s, h = g.k // 2 % 2, HC * (g.k % 2) + j, HC * (g.k % NCH) + j
                if j == 0:
                    if g.is_first():
                        pe.wait_ge(const_dve, 1)
                    pe.wait_ge(z_in[i], g.over(4, 1, 16 * Z_DMAS))
                    pe.wait_ge(shift_ready, g.over(1, 1))
                    if g.k % NCH == 0:
                        pe.wait_ge(ksv_in[g.k // NCH % 2], g.over(PAIR, 1, 16 * KSV_DMAS))
                at_least(pe, prob_ready, g.over(1, 0, HC) + j - 1)
                if j == 0:
                    newest = g.back(LAG_ROWMAX - LAG_SCORE + 1)
                    pe.wait_ge(max_ready, newest.over(1, 1, QT) if newest.valid(NG) else NG * QT)
                nc.tensor.matmul(p_s[j % 2][0:S2, :], ks[0:KR, g.k // NCH % 2, h, :], z[0:KR, i, s, :],
                                 start=True, stop=True).then_inc(s_summed, 1)

            def values(g):
                pe.wait_ge(prob_ready, g.over(1, 1, HC))
                at_least(pe, cx_ready, g.over(1))
                for j in range(HC):
                    h = HC * (g.k % NCH) + j
                    nc.tensor.matmul(p_v[DK * j:DK * (j + 1), :], vb[0:S2, g.k // NCH % 2, DK * h:DK * (h + 1)],
                                     prob[0:S2, j, :], start=True, stop=True)
                for j in range(HC):
                    last = nc.tensor.matmul(p_d[DK * j:DK * (j + 1), :], ones[0:S2, :], prob[0:S2, j, :],
                                            start=True, stop=True)
                last.then_inc(pv_summed, 1)

            def project_out(m, kc):
                i, t = m.k // QT % 2, m.k % QT
                if kc == 0:
                    if t == 0:
                        pe.wait_ge(ch_ready, m.over(QT, 1, KC))
                        pe.wait_ge(cl_ready, m.over(QT, 1, KC))
                    at_least(pe, y_ready, m.over(1))
                for n, (x, w) in enumerate(((ch, woh), (ch, wol), (cl, woh))):
                    last = nc.tensor.matmul(p_o[:], x[:, i, kc, P * t:P * (t + 1)], w[:, kc, :],
                                            start=(kc == 0 and n == 0), stop=(kc == KC - 1 and n == 2))
                if kc == KC - 1:
                    last.then_inc(o_summed, 1)

            def project_last(c):
                pe.wait_ge(ch_ready, NG - NCH + c + 1)
                pe.wait_ge(cl_ready, NG - NCH + c + 1)
                steps = [(t, c) for t in range(QT - 1)]
                if c >= NCH - 2:
                    steps += [(QT - 1, kc) for kc in (range(NCH - 1) if c == NCH - 2 else (c,))]
                for t, kc in steps:
                    bank, left, count = last_banks[t]
                    if kc == 0:
                        pe.wait_ge(left, count)
                    for n, (x, w) in enumerate(((ch, woh), (ch, wol), (cl, woh))):
                        last = nc.tensor.matmul(bank[:], x[:, (B - 1) % 2, kc, P * t:P * (t + 1)], w[:, kc, :],
                                                start=(kc == 0 and n == 0), stop=(kc == KC - 1 and n == 2))
                    if kc == KC - 1:
                        last.then_inc(o_summed, 1)

            def slot(g):
                q, r, s, v, o = g, g.back(LAG_ROWMAX), g.back(LAG_SCORE), g.back(LAG_PV), g.back(LAG_OUT)
                if v.valid(NG):
                    values(v)
                if g.k % 2 == 1 and g.back(3).valid(NG):
                    turn_maxima(g.back(3))
                if s.valid(NG):
                    scores(s, 0)
                    scores(s, 1)
                spread = not o.valid(NS)
                for t in range(QT):
                    if q.valid(NG):
                        project_q(q, t)
                    if s.valid(NG) and t % 2 == 1:
                        scores(s, 2 + t // 2)
                    if r.valid(NG) and (spread or t % 2 == 1):
                        rowmax_scores(r, t if spread else t // 2)
                for t in range(QT):
                    if o.valid(NS):
                        project_out(o, t)
                        if r.valid(NG) and t < 2:
                            rowmax_scores(r, 2 + t)
                c = last_batch_chunk(g, LAG_PV + 1)
                if c is not None:
                    project_last(c)
            run(pe, slot)
            project_last(NCH - 1)

        @block.scalar
        def _(act):
            def exp(g, j):
                act.wait_ge(s_summed, g.over(1, 0, HC) + j + 1)
                if j == 0:
                    at_least(act, pv_summed, g.over(1))
                nc.scalar.activation(prob[0:S2, j, :], p_s[j % 2][0:S2, :], ACT.Exp, scale=SCALE).then_inc(prob_ready, 1)

            def split_x_high(n):
                i = n.k // KC % 2
                act.wait_ge(xt_in[n.k % 2], n.over(2, 1, 16))
                if n.k % KC == 0:
                    at_least(act, q_summed, n.over(KC, -1, NCH))
                nc.scalar.copy(xh[:, i, n.k % KC, :], xt[:, n.k % 2, :]).then_inc(xh_ready, 1)

            def place_maxima(g, cc):
                i = g.k // 2 % 2
                if cc == 0:
                    act.wait_ge(t_done, g.over(2, 1))
                    at_least(act, s_summed, g.over(2, -1, HALF))
                nc.scalar.copy(z[QI:KR, i, HC * cc:HC * (cc + 1), :],
                               p_t[0:HALF, :].unsqueeze(1).broadcast_to([HALF, HC, S])).then_inc(shift_ready, 1)

            def q_high(g):
                i = g.k // 2 % 2
                act.wait_ge(q_summed, g.over(1, 1))
                at_least(act, a_summed, g.over(1, -3, QT))
                if g.k % 2 == 0:
                    at_least(act, z_in[i], g.over(4, 0, 16 * Z_DMAS))
                nc.scalar.activation(qh[:, i, g.k % 2, :], p_q[:], ACT.Identity,
                                     bias=bq_col[:, g.k % NCH:g.k % NCH + 1]).then_inc(qh_ready, 1)

            def ctx_high(g):
                i = g.k // NCH % 2
                act.wait_ge(cx_ready, g.over(1, 1))
                if g.k % NCH == 0:
                    at_least(act, o_summed, g.over(NCH, -1, QT))
                nc.scalar.copy(ch[:, i, g.k % NCH, :], cx[:, g.k % 2, :]).then_inc(ch_ready, 1)

            def normalize(m):
                i = m.k % 4
                act.wait_ge(nmr_ready, m.over(1, 1))
                nc.scalar.activation(rows(m), rows(m), ACT.Identity, bias=nmr[:, i, :],
                                     scale=rstd[:, i, :]).then_inc(normed, 1)

            def slot(g):
                s, v, m, n = g.back(LAG_SCORE), g.back(LAG_PV), g.back(LAG_NORM), g.back(LAG_SPLIT)
                turn = g.k % 2 == 1 and g.back(3).valid(NG)
                if s.valid(NG):
                    exp(s, 0)
                    exp(s, 1)
                if n.valid(NG):
                    split_x_high(n)
                if s.valid(NG):
                    exp(s, 2)
                if g.valid(NG):
                    q_high(g)
                if s.valid(NG):
                    exp(s, 3)
                if turn:
                    place_maxima(g.back(3), 0)
                if v.valid(NG):
                    ctx_high(v)
                if m.valid(NS):
                    normalize(m)
                if turn:
                    place_maxima(g.back(3), 1)
            run(act, slot)
            for m in range(NG + LAG_PV - LAG_NORM, NS + ON_POOL):
                normalize(Slot(0, m))

        @block.vector
        def _(dve):
            for i in range(2):
                for hf in range(2):
                    last = nc.vector.tensor_copy(ks[QI:KR, i, HALF * hf:HALF * (hf + 1), :],
                                                 ident[0:HALF, 0:HALF].unsqueeze(2).broadcast_to([HALF, HALF, S2]))
            last.then_inc(const_dve, 1)

            def add_residual(m):
                i = m.k % 4
                dve.wait_ge(o_summed, m.over(1, 1))
                dve.wait_ge(xb_ready, m.over(1, 1))
                at_least(dve, stored[i], m.over(4, 0, 16))
                nc.vector.tensor_tensor(y[:, i, :], p_o[:], xn[:, m.k % 2, :], ALU.add).then_inc(y_ready, 1)
                dve.wait_ge(y_ready, m.over(1, 1))
                nc.vector.bn_stats(stats[:, i, :], y[:, i, :]).then_inc(stats_ready, 1)

            def invert_sums(g):
                dve.wait_ge(pv_summed, g.over(1, 1))
                nc.vector.reciprocal(rden[:], p_d[:]).then_inc(rden_ready, 1)

            def variance(m):
                i = m.k % 4
                nc.vector.bn_aggr(mv[:, i, :], stats[:, i, :]).then_inc(mv_ready, 1)
                dve.wait_ge(mv_ready, m.over(1, 1))
                nc.vector.tensor_scalar(ve[:, i, :], mv[:, i, 1:2], EPS, None, ALU.add).then_inc(ve_ready, 1)

            def divide(g):
                i = g.k % 2
                dve.wait_ge(rden_ready, g.over(1, 1))
                at_least(dve, ch_ready, g.over(1, -1))
                at_least(dve, cl_ready, g.over(1, -1))
                nc.vector.tensor_tensor(cx[:, i, :], p_v[:], rden[:], ALU.mult).then_inc(cx_ready, 1)

            def mean_over_std(m):
                i = m.k % 4
                dve.wait_ge(rstd_ready, m.over(1, 1))
                nc.vector.scalar_tensor_tensor(out=nmr[:, i, :], in0=mv[:, i, 0:1], scalar=-1.0, in1=rstd[:, i, :],
                                               op0=ALU.mult, op1=ALU.mult).then_inc(nmr_ready, 1)

            def q_low(g):
                i = g.k // 2 % 2
                dve.wait_ge(qh_ready, g.over(1, 1))
                if g.k % 2 == 0:
                    at_least(dve, z_in[i], g.over(4, 0, 16 * Z_DMAS))
                nc.vector.scalar_tensor_tensor(
                    out=ql[:, i, g.k % 2, :], in0=p_q[:], scalar=bq_col[:, g.k % NCH:g.k % NCH + 1],
                    in1=qh[:, i, g.k % 2, :].bitcast(F32), op0=ALU.add, op1=ALU.subtract).then_inc(ql_ready, 1)

            def row_maxima(g, t):
                i = g.k // 2 % 2
                dve.wait_ge(a_summed, g.over(1, 0, QT) + t + 1)
                if t == 0 and g.k % 2 == 0:
                    at_least(dve, t_done, g.over(2, -1))
                nc.vector.tensor_reduce(nm[:, i, t, HC * (g.k % 2):HC * (g.k % 2 + 1)],
                                        p_a[t % 2][:, 0:HC * S2].rearrange("p (h k) -> p h k", k=S2),
                                        AX_X, ALU.max, negate=True).then_inc(max_ready, 1)

            def slot(g):
                r, v, m = g.back(LAG_ROWMAX), g.back(LAG_PV), g.back(LAG_NORM)
                if m.valid(NS):
                    add_residual(m)
                    dve.wait_ge(stats_ready, m.over(1, 1))
                if v.valid(NG):
                    invert_sums(v)
                if r.valid(NG):
                    row_maxima(r, 0)
                if v.valid(NG):
                    divide(v)
                if m.valid(NS):
                    variance(m)
                if r.valid(NG):
                    row_maxima(r, 1)
                if g.valid(NG):
                    q_low(g)
                if r.valid(NG):
                    row_maxima(r, 2)
                    row_maxima(r, 3)
                if m.valid(NS):
                    mean_over_std(m)
            run(dve, slot)

            def add_last(t):
                dve.wait_ge(o_summed, NS + t + 1)
                dve.wait_ge(xb_last_ready, t + 1)
                nc.vector.tensor_tensor(x_last[t], last_banks[t][0][:], x_last[t], ALU.add).then_inc(y_ready, 1)
                dve.wait_ge(y_ready, NS + t + 1)
                nc.vector.bn_stats(stats[:, t, :], x_last[t]).then_inc(stats_ready, 1)
                dve.wait_ge(stats_ready, NS + t + 1)
                variance(Slot(0, NS + t))

            def center_scale(t):
                nc.vector.scalar_tensor_tensor(out=x_last[t], in0=x_last[t], scalar=mv[:, t, 0:1], in1=gamma[:],
                                               op0=ALU.subtract, op1=ALU.mult).then_inc(y_last_scaled, 1)

            def divide_shift(t):
                dve.wait_ge(rstd_ready, NS + t + 1)
                dve.wait_ge(y_last_scaled, t - ON_POOL + 1)
                nc.vector.scalar_tensor_tensor(out=x_last[t], in0=x_last[t], scalar=rstd[:, t, :], in1=beta[:],
                                               op0=ALU.mult, op1=ALU.add).then_inc(y_last_done, 1)

            m = Slot(0, NS - 1)
            add_residual(m)
            dve.wait_ge(stats_ready, NS)
            variance(m)
            add_last(0)
            mean_over_std(m)
            add_last(1)
            mean_over_std(Slot(0, NS))
            add_last(2)
            mean_over_std(Slot(0, NS + 1))
            center_scale(2)
            add_last(3)
            divide_shift(2)
            center_scale(3)
            divide_shift(3)

        @block.gpsimd
        def _(pool):
            nc.gpsimd.memset(kb[1][:].bitcast(F32), 0.0).then_inc(kb1_zeroed, 1)

            def split_x_low(n):
                i = n.k // KC % 2
                pool.wait_ge(xh_ready, n.over(1, 1))
                nc.gpsimd.tensor_tensor(xl[:, i, n.k % KC, :], xt[:, n.k % 2, :],
                                        xh[:, i, n.k % KC, :].bitcast(F32), ALU.subtract).then_inc(xl_ready, 1)

            def inverse_std(m):
                i = m.k % 4
                pool.wait_ge(ve_ready, m.over(1, 1))
                nc.gpsimd.tensor_tensor(rstd[:, i, :], ve[:, i, :], minus_half[:], ALU.pow).then_inc(rstd_ready, 1)

            def scale(m):
                pool.wait_ge(normed, m.over(1, 1))
                nc.gpsimd.tensor_tensor(rows(m), rows(m), gamma[:], ALU.mult).then_inc(scaled, 1)

            def shift(m):
                pool.wait_ge(scaled, m.over(1, 1))
                nc.gpsimd.tensor_tensor(rows(m), rows(m), beta[:], ALU.add).then_inc(y_done, 1)

            def ctx_low(g):
                i = g.k // NCH % 2
                pool.wait_ge(ch_ready, g.over(1, 1))
                nc.gpsimd.tensor_tensor(cl[:, i, g.k % NCH, :], cx[:, g.k % 2, :],
                                        ch[:, i, g.k % NCH, :].bitcast(F32), ALU.subtract).then_inc(cl_ready, 1)

            def add_bo(m):
                if m.is_first():
                    pool.wait_ge(rows_in, 48)
                pool.wait_ge(xn_in[m.k % 2], m.over(2, 1, 16))
                nc.gpsimd.tensor_tensor(xn[:, m.k % 2, :], xn[:, m.k % 2, :], bo[:], ALU.add).then_inc(xb_ready, 1)

            def add_bo_last(t):
                pool.wait_ge(x_last_in[t], 16)
                nc.gpsimd.tensor_tensor(x_last[t], x_last[t], bo[:], ALU.add).then_inc(xb_last_ready, 1)

            def slot(g):
                v, m, n, b = g.back(LAG_PV), g.back(LAG_NORM), g.back(LAG_SPLIT), g.back(LAG_NORM - 1)
                if g.back(LAG_SCALE).valid(NS):
                    scale(g.back(LAG_SCALE))
                    shift(g.back(LAG_SCALE))
                if n.valid(NG):
                    split_x_low(n)
                if b.valid(NS):
                    add_bo(b)
                if m.valid(NS):
                    inverse_std(m)
                if v.valid(NG):
                    ctx_low(v)
                t = last_batch_chunk(g, LAG_PV)
                if t is not None:
                    add_bo_last(t)
            run(pool, slot)

            last = [Slot(0, NS + t) for t in range(-2, QT)]
            scale(last[0])
            inverse_std(last[1])
            shift(last[0])
            inverse_std(last[2])
            scale(last[1])
            inverse_std(last[3])
            shift(last[1])
            inverse_std(last[4])
            scale(last[2])
            inverse_std(last[5])
            shift(last[2])
            scale(last[3])
            shift(last[3])


def xattn(nc, a, out):
    B, S, _ = a["x"].shape
    S2 = a["ctx_t"].shape[1] // B
    kh_dram = nc.dram_tensor("k_high", (D, B * S2), F32, kind="Internal").ap()
    kl_dram = nc.dram_tensor("k_low", (D, B * S2), F32, kind="Internal").ap()
    v_dram = nc.dram_tensor("v_all", (B, S2, D), F32, kind="Internal").ap()
    with ExitStack() as ctx:
        keep = {n: ctx.enter_context(nc.sbuf_tensor(n, [P, KC, D], F32R)) for n in ("wqh", "wql", "woh", "wol")}
        for n, shape, dt in (("bq_col", [P, KC], F32),
                             ("xt", [P, 2, S], F32),
                             ("xh", [P, 2, KC, S], F32R),
                             ("xl", [P, 2, KC, S], F32R),
                             ("y", [P, 4, D], F32),
                             ("kb0", [P, NCH, HC * S2], F32R),
                             ("ident", [P, P], F32), ("ones", [P, DK], F32), ("minus_half", [P, 1], F32)):
            keep[n] = ctx.enter_context(nc.sbuf_tensor(n, shape, dt))
        for n in ("xh_ready", "xl_ready", "const_pool", "kb0_zeroed"):
            keep[n] = ctx.enter_context(nc.semaphore(n))
        for n, count in (("xt_in", 2), ("v_stored", 4), ("kb_in", 2)):
            keep[n] = [ctx.enter_context(nc.semaphore(f"{n}{i}")) for i in range(count)]
        bq_in = ctx.enter_context(nc.semaphore("bq_in"))
        with nc.Block() as block:
            @block.sync
            def _(sp):
                sp.dma_start(keep["bq_col"][:], a["bq"]).then_inc(bq_in, 16)
                sp.wait_ge(bq_in, 16)
        project_context(nc, a, keep, kh_dram, kl_dram, v_dram.rearrange("b k d -> (b k) d"), B, S2)
        attend(nc, a, keep, kh_dram, kl_dram, v_dram, out, B, S, S2)


def kernel(**inputs):
    import numpy as np
    import concourse.bacc as bacc
    from concourse.bass_utils import run_bass_kernel_spmd

    x = np.ascontiguousarray(inputs["x"])
    context = np.asarray(inputs["ctx_1024"])
    w = {n: np.asarray(inputs[f"L0_xattn_{n}"])
         for n in ("Wq", "bq", "Wk", "bk", "Wv", "bv", "Wo", "bo", "ln_gamma", "ln_beta")}
    arrays = {"x": x, "x_t": np.ascontiguousarray(x.transpose(0, 2, 1)),
              "ctx_t": np.ascontiguousarray(context.reshape(-1, D).T)}
    for n, v in w.items():
        arrays[n] = np.ascontiguousarray(v.reshape(KC, P).T if n in ("bq", "bk") else v)
    nc = bacc.Bacc("TRN2", target_bir_lowering=False, num_devices=1)
    a = {n: nc.dram_tensor(f"in_{n}", v.shape, mybir.dt.from_np(v.dtype), kind="ExternalInput").ap()
         for n, v in arrays.items()}
    out = nc.dram_tensor("out_0_dram", x.shape, F32, kind="ExternalOutput").ap()
    xattn(nc, a, out)
    r = run_bass_kernel_spmd(nc, [{f"in_{n}": v for n, v in arrays.items()}], core_ids=[0])
    return r.results[0]["out_0_dram"]
```

```python
from contextlib import ExitStack

import concourse.bass as bass
from concourse import mybir

F32 = mybir.dt.float32
F32R = mybir.dt.float32r
ALU = mybir.AluOpType
ACT = mybir.ActivationFunctionType
AX_X = mybir.AxisListType.X

P = 128
D = 512
KC = D // P
DK = 32
HC = P // DK
NCH = D // P
HALF = 2 * HC
PAIR = 2 * NCH
EPS = 1e-5

LAG_SPLIT = -4
LAG_LOAD_X = -5
LAG_ROWMAX = 1
LAG_PV = 5
LAG_SCORE = 4
LAG_OUT = 9
LAG_NORM = 10
LAG_SCALE = 11
LAG_STORE = 12

V_FIRST = 4
V_SLOTS = (0, 1, 1, 2, 3, 3)


class Slot:

    def __init__(self, u, k):
        self.u, self.k = u, k

    def back(self, lag):
        return Slot(self.u, self.k - lag)

    def over(self, d, plus=0, times=1):
        return self.u * (PAIR // d * times) + (self.k // d + plus) * times

    def valid(self, n):
        return not isinstance(self.u, int) or 0 <= PAIR * self.u + self.k < n

    def is_first(self):
        return isinstance(self.u, int) and PAIR * self.u + self.k == 0


def at_least(engine, sem, value):
    if not isinstance(value, int) or value > 0:
        engine.wait_ge(sem, value)


def all_at_least(engine, *waits):
    for _, value in waits:
        if not isinstance(value, int):
            engine.compute_val(value)
    for sem, value in waits:
        at_least(engine, sem, value)


def v_tiles(B, S2):
    return [(r, min(P, B * S2 - r)) for r in range(0, B * S2, P)]


def v_products(nc, keep, bank, parts, r, m):
    (cxh, cxl), wvh, wvl = parts, keep["wvh"], keep["wvl"]
    for kc in range(KC):
        for n, (x, w) in enumerate(((cxh, wvh), (cxh, wvl), (cxl, wvh))):
            last = nc.tensor.matmul(bank[0:m, :], x[:, kc, r:r + m], w[:, kc, :],
                                    start=(kc == 0 and n == 0), stop=(kc == KC - 1 and n == 2))
    return last


def project_context(nc, a, keep, kh_dram, kl_dram, v_dram, B, S2):
    NK = B * S2
    NT = 3
    N1 = V_FIRST * P
    cuts = [0, N1, N1 + (NK - N1) // 4 * 2, NK]
    tiles_k = [(c, cuts[i], cuts[i + 1]) for c in range(KC) for i in range(NT)]
    tiles_v = v_tiles(B, S2)[:V_FIRST]
    PK = 2 * NT
    CX = 3
    xt, xh, xl, y, wvh, wvl, bv_row = (keep[n] for n in ("xt", "xh", "xl", "y", "wvh", "wvl", "bv_row"))
    xt_in, xh_ready, xl_ready, v_stored, v_summed, v_out, const_pool = (
        keep[n] for n in ("xt_in", "xh_ready", "xl_ready", "v_stored", "v_summed", "v_out", "const_pool"))
    with ExitStack() as ctx:
        def sb(name, shape, dt):
            return ctx.enter_context(nc.sbuf_tensor(name, shape, dt))

        def sem(name):
            return ctx.enter_context(nc.semaphore(name))

        cx = sb("cx", [P, CX, NK], F32)
        cx1 = [sb(n, [P, KC, N1], F32R) for n in ("cx1h", "cx1l")]
        cx2 = keep["cx2"]
        w_raw = [sb(f"w_raw{i}", [P, KC, D], F32) for i in range(2)]
        wkh, wkl = sb("wkh", [P, KC, D], F32R), sb("wkl", [P, KC, D], F32R)
        kth, ktl = sb("kth", [P, 2, NK], F32R), sb("ktl", [P, 2, NK], F32R)
        bk_col = sb("bk_col", [P, KC], F32)
        pk = [ctx.enter_context(nc.psum_tensor(f"pk{i}", [P, D], F32)) for i in range(PK)]
        pv = [ctx.enter_context(nc.psum_tensor(f"pvv{i}", [P, D], F32)) for i in range(2)]

        wk_in, cx_in = ([sem(f"{n}_in{i}") for i in range(KC)] for n in ("wk", "cx"))
        biases_in, wv_in, wq_in = (sem(n) for n in ("biases_in", "wv_in", "wq_in"))
        kv_high, kv_low, q_high, q_low = (sem(n) for n in ("kv_high", "kv_low", "wq_high", "wq_low"))
        k_summed, k_high_out, k_low_out = sem("k_summed"), sem("k_high_out"), sem("k_low_out")
        k_stored = [sem(f"k_stored{i}") for i in range(2)]
        first = [part for kc in range(KC) for part in (
            (w_raw[0][:, kc, :], wkh[:, kc, :], wkl[:, kc, :]),
            (cx[:, kc % CX, 0:N1], cx1[0][:, kc, :], cx1[1][:, kc, :]),
            (cx[:, kc % CX, N1:NK], cx2[0][:, kc, :], cx2[1][:, kc, :]))]
        first += [(w_raw[1][:, kc, :], wvh[:, kc, :], wvl[:, kc, :]) for kc in range(KC)]
        second = [(w_raw[0][:, kc, :], keep["wqh"][:, kc, :], keep["wql"][:, kc, :]) for kc in range(KC)]

        with nc.Block() as block:
            @block.sync
            def _(sp):
                def load_xt(n):
                    if n >= 2:
                        sp.wait_ge(xh_ready, n - 1)
                        sp.wait_ge(xl_ready, n - 1)
                    sp.dma_start(xt[:, n % 2, :], a["x_t"][0, P * n:P * (n + 1), :]).then_inc(xt_in[n % 2], 16)

                def by_chunk(w):
                    return w.rearrange("(c p) n -> p c n", p=P)

                for kc in range(KC):
                    sp.dma_start(w_raw[0][:, kc, :], a["Wk"][P * kc:P * (kc + 1), :]).then_inc(wk_in[kc], 16)
                    if kc >= CX:
                        sp.wait_ge(kv_high, 3 * (kc - CX) + 3)
                        sp.wait_ge(kv_low, 3 * (kc - CX) + 3)
                    sp.dma_start(cx[:, kc % CX, :], a["ctx_t"][P * kc:P * (kc + 1), :]).then_inc(cx_in[kc], 16)
                sp.dma_start(bk_col[:], a["bk"]).then_inc(biases_in, 16)
                sp.dma_start(keep["bq_col"][:], a["bq"]).then_inc(keep["bq_in"], 16)
                sp.dma_start(bv_row[:], a["bv"].partition_broadcast(P)).then_inc(biases_in, 16)
                sp.dma_start(w_raw[1][:], by_chunk(a["Wv"])).then_inc(wv_in, 16)
                load_xt(0)
                load_xt(1)
                sp.wait_ge(kv_high, 3 * KC)
                sp.wait_ge(kv_low, 3 * KC)
                sp.dma_start(w_raw[0][:], by_chunk(a["Wq"])).then_inc(wq_in, 16)

                for c in range(KC):
                    sp.wait_ge(k_high_out, NT * (c + 1))
                    sp.wait_ge(k_low_out, NT * (c + 1))
                    for t, dst in ((kth, kh_dram), (ktl, kl_dram)):
                        sp.dma_start(dst[P * c:P * (c + 1), :], t[:, c % 2, :].bitcast(F32)).then_inc(k_stored[c % 2], 16)
                    if c == 1:
                        load_xt(2)
                        load_xt(3)
                for i in range(2):
                    sp.wait_ge(k_stored[i], 16 * KC)
                sp.wait_ge(keep["kb0_zeroed"], 1)
                src = kh_dram.rearrange("(c j d) (b k) -> b j d c k", j=HC, d=DK, k=S2)[0]
                for j in range(HC):
                    sp.dma_start(keep["kb0"][DK * j:DK * (j + 1), :, S2 * j:S2 * (j + 1)].bitcast(F32),
                                 src[j]).then_inc(keep["kb_in"][0], 16)
                for i, (r, n) in enumerate(tiles_v):
                    sp.wait_ge(v_out, i + 1)
                    sp.dma_start(v_dram[r:r + n, :], y[0:n, i % 4, :]).then_inc(v_stored[i % 4], 16)

            @block.scalar
            def _(act):
                def high(part, signal):
                    raw, hi, _ = part
                    nc.scalar.copy(hi, raw).then_inc(signal, 1)

                def k_high(i):
                    c, lo, hi = tiles_k[i]
                    act.wait_ge(k_summed, i + 1)
                    if c >= 2:
                        act.wait_ge(k_stored[c % 2], 32)
                    nc.scalar.activation(kth[:, c % 2, lo:hi], pk[i % PK][:, 0:hi - lo], ACT.Identity,
                                         bias=bk_col[:, c:c + 1]).then_inc(k_high_out, 1)

                def x_high(n):
                    act.wait_ge(xt_in[n % 2], 16 * (n // 2 + 1))
                    nc.scalar.copy(xh[:, 0, n, :], xt[:, n % 2, :]).then_inc(xh_ready, 1)

                for kc in range(KC):
                    act.wait_ge(wk_in[kc], 16)
                    high(first[3 * kc], kv_high)
                    act.wait_ge(cx_in[kc], 16)
                    high(first[3 * kc + 1], kv_high)
                    high(first[3 * kc + 2], kv_high)
                act.wait_ge(biases_in, 32)
                for i in range(PK):
                    k_high(i)
                act.wait_ge(wv_in, 16)
                for kc in range(KC):
                    high(first[3 * KC + kc], kv_high)
                x_high(0)
                x_high(1)
                act.wait_ge(wq_in, 16)
                for i in range(PK, 2 * PK):
                    k_high(i)
                    if i - PK < KC:
                        high(second[i - PK], q_high)
                x_high(2)
                x_high(3)

            @block.vector
            def _(dve):
                def low(i):
                    raw, hi, lo = first[i]
                    dve.wait_ge(kv_high, i + 1)
                    nc.vector.tensor_tensor(lo, raw, hi.bitcast(F32), ALU.subtract).then_inc(kv_low, 1)

                def k_low(i):
                    c, lo, hi = tiles_k[i]
                    dve.wait_ge(k_high_out, i + 1)
                    if c >= 2:
                        dve.wait_ge(k_stored[c % 2], 32)
                    nc.vector.scalar_tensor_tensor(
                        out=ktl[:, c % 2, lo:hi], in0=pk[i % PK][:, 0:hi - lo], scalar=bk_col[:, c:c + 1],
                        in1=kth[:, c % 2, lo:hi].bitcast(F32), op0=ALU.add, op1=ALU.subtract).then_inc(k_low_out, 1)

                for i in range(3 * KC):
                    low(i)
                dve.wait_ge(biases_in, 32)
                for i in range(PK):
                    k_low(i)
                for kc in range(KC):
                    low(3 * KC + kc)
                for i in range(PK, 2 * PK):
                    k_low(i)
                for i, (r, n) in enumerate(tiles_v):
                    dve.wait_ge(v_summed, i + 1)
                    if i >= 4:
                        dve.wait_ge(v_stored[i % 4], 16 * (i // 4))
                    nc.vector.tensor_tensor(y[0:n, i % 4, :], pv[i % 2][0:n, :], bv_row[0:n, :],
                                            ALU.add).then_inc(v_out, 1)

            @block.gpsimd
            def _(pool):
                ident = keep["ident"]
                nc.gpsimd.memset(ident[:], 0.0).then_inc(const_pool, 1)
                nc.gpsimd.memset(keep["kb0"][:].bitcast(F32), 0.0).then_inc(keep["kb0_zeroed"], 1)
                nc.gpsimd.memset(keep["ones"][:], 1.0)
                nc.gpsimd.memset(keep["minus_half"][:], -0.5)
                pool.wait_ge(const_pool, 1)
                nc.gpsimd.affine_select(out=ident[:], in_=ident[:], compare_op=ALU.not_equal, fill=1.0, base=0,
                                        pattern=[[-1, P]], channel_multiplier=1).then_inc(const_pool, 1)

                def x_low(n):
                    pool.wait_ge(xh_ready, n + 1)
                    nc.gpsimd.tensor_tensor(xl[:, 0, n, :], xt[:, n % 2, :], xh[:, 0, n, :].bitcast(F32),
                                            ALU.subtract).then_inc(xl_ready, 1)

                x_low(0)
                x_low(1)
                for i, (raw, hi, lo) in enumerate(second):
                    pool.wait_ge(q_high, i + 1)
                    nc.gpsimd.tensor_tensor(lo, raw, hi.bitcast(F32), ALU.subtract).then_inc(q_low, 1)
                x_low(2)
                x_low(3)

            @block.tensor
            def _(pe):
                def k_products(i, kc):
                    c, lo, hi = tiles_k[i]
                    (cxh, cxl), at = (cx1, lo) if hi <= N1 else (cx2, lo - N1)
                    for n, (w, x) in enumerate(((wkh, cxh), (wkh, cxl), (wkl, cxh))):
                        last = nc.tensor.matmul(pk[i % PK][:, 0:hi - lo], w[:, kc, P * c:P * (c + 1)],
                                                x[:, kc, at:at + hi - lo],
                                                start=(kc == 0 and n == 0), stop=(kc == KC - 1 and n == 2))
                    if kc == KC - 1:
                        last.then_inc(k_summed, 1)

                for kc in range(KC):
                    for i in range(PK):
                        if i < 2:
                            pe.wait_ge(kv_low, 3 * kc + 2 + i)
                        k_products(i, kc)
                for i in range(PK, 2 * PK):
                    pe.wait_ge(k_low_out, i - PK + 1)
                    for kc in range(KC):
                        k_products(i, kc)
                pe.wait_ge(kv_low, 4 * KC)
                for i, (r, m) in enumerate(tiles_v):
                    if i >= 2:
                        pe.wait_ge(v_out, i - 1)
                    v_products(nc, keep, pv[i % 2], cx1, r, m).then_inc(v_summed, 1)


def attend(nc, a, keep, kh_dram, kl_dram, v_dram, out, B, S, S2):
    NG = B * NCH
    QT = S // P
    NM = B * QT
    NS = NM - QT
    assert QT == NCH and B % 2 == 0
    SCALE = float(DK) ** -0.5
    QI = 3 * DK
    KR = QI + HALF
    wqh, wql, woh, wol, bq_col = (keep[n] for n in ("wqh", "wql", "woh", "wol", "bq_col"))
    xt, xh, xl, y, ident, ones, minus_half, bv_row = (
        keep[n] for n in ("xt", "xh", "xl", "y", "ident", "ones", "minus_half", "bv_row"))
    ch, cl = keep["ch"], keep["cl"]
    xt_in, xh_ready, xl_ready, v_stored, v_summed, v_out = (
        keep[n] for n in ("xt_in", "xh_ready", "xl_ready", "v_stored", "v_summed", "v_out"))
    tiles_v = v_tiles(B, S2)
    VT = len(tiles_v)
    assert VT <= V_FIRST + len(V_SLOTS) and max(V_SLOTS) < LAG_PV
    xt_dram = a["x_t"].rearrange("b (c p) s -> (b c) p s", p=P)
    x_dram = a["x"].rearrange("b (t p) d -> (b t) p d", p=P)
    out_dram = out.rearrange("b (t p) d -> (b t) p d", p=P)
    with ExitStack() as ctx:
        def sb(name, shape, dt):
            return ctx.enter_context(nc.sbuf_tensor(name, shape, dt))

        def psum(name):
            return ctx.enter_context(nc.psum_tensor(name, [P, 512], F32))

        def sem(name):
            return ctx.enter_context(nc.semaphore(name))

        qh, ql = (sb(n, [P, 2, 2, S], F32R) for n in ("qh", "ql"))
        z = sb("z", [P, 2, HALF, S], F32R)
        ks = sb("ks", [P, 2, NCH * HC, S2], F32R)
        kb = [keep["kb0"], sb("kb1", [P, NCH, HC * S2], F32R)]
        vb = sb("vb", [P, 2, D], F32)
        nm = sb("nm", [P, 2, QT, HALF], F32)
        prob = sb("prob", [P, HC, S], F32)
        rden = sb("rden", [P, S], F32)
        cx = sb("cxt", [P, 2, S], F32)
        xn = sb("xn", [P, 2, D], F32)
        gamma, beta, bo = (sb(n, [P, D], F32) for n in ("gamma_row", "beta_row", "bo_row"))
        stats = sb("stats", [P, 4, 6], F32)
        mv = sb("mv", [P, 4, 2], F32)
        ve, rstd, nmr = (sb(n, [P, 4, 1], F32) for n in ("ve", "rstd", "nmr"))
        p_q, p_t, p_v, p_d, p_o = (psum(n) for n in ("p_q", "p_t", "p_v", "p_d", "p_o"))
        p_s = [psum(f"p_s{i}") for i in range(2)]
        p_a = [psum("p_a"), p_s[0]]

        xn_in = [sem(f"xn_in{i}") for i in range(2)]
        kb_in = keep["kb_in"]
        ks_in = [sem(f"ks_in{i}") for i in range(2)]
        vb_in = [sem(f"vb_in{i}") for i in range(2)]
        wo_in = [sem(f"wo_in{i}") for i in range(2)]
        z_in = [sem(f"z_in{i}") for i in range(2)]
        stored = [sem(f"stored{i}") for i in range(4)]
        rows_in = sem("rows_in")
        x_last_in = [sem(f"x_last_in{t}") for t in range(QT)]
        q_summed, a_summed, t_done, s_summed, pv_summed, o_summed = (
            sem(n) for n in ("q_summed", "a_summed", "t_done", "s_summed", "pv_summed", "o_summed"))
        wo_high, qh_ready, shift_ready, prob_ready, ch_ready, normed = (
            sem(n) for n in ("wo_high", "qh_ready", "shift_ready", "prob_ready", "ch_ready", "normed"))
        ql_ready, max_ready, rden_ready, cx_ready, y_ready, stats_ready = (
            sem(n) for n in ("ql_ready", "max_ready", "rden_ready", "cx_ready", "y_ready", "stats_ready"))
        mv_ready, ve_ready, nmr_ready, const_dve, y_last_scaled, y_last_done = (
            sem(n) for n in ("mv_ready", "ve_ready", "nmr_ready", "const_dve", "y_last_scaled", "y_last_done"))
        xb_ready, rstd_ready, scaled, y_done, cl_ready, kb1_zeroed, xb_last_ready, wo_low = (
            sem(n) for n in ("xb_ready", "rstd_ready", "scaled", "y_done", "cl_ready", "kb1_zeroed",
                             "xb_last_ready", "wo_low"))
        Z_DMAS, KB_DMAS, KS_DMAS = 3 * HC, HC, 3

        last_banks = [(p_q, ql_ready, NG), (p_a[0], max_ready, NG * QT), (p_t, shift_ready, NG),
                      (p_s[0], prob_ready, NG * HC)]
        x_last = [xt[:, 0, :], xt[:, 1, :], vb[:, B % 2, :], bv_row[:]]
        ON_POOL = 2

        def rows(m):
            if isinstance(m.u, int) and PAIR * m.u + m.k >= NS:
                return x_last[m.k % QT]
            return y[:, m.k % 4, :]

        def last_batch_chunk(g, lag):
            if isinstance(g.u, int) and 0 <= PAIR * g.u + g.k - lag - (NG - NCH) < NCH:
                return PAIR * g.u + g.k - lag - (NG - NCH)
            return None

        def v_in_slot(g):
            if not isinstance(g.u, int):
                return []
            return [V_FIRST + n for n, k in enumerate(V_SLOTS[:VT - V_FIRST]) if k == PAIR * g.u + g.k]

        def wo_in_slot(g):
            for half in range(2):
                if g.back(LAG_PV + 2 * half).is_first():
                    return [2 * half, 2 * half + 1]
            return []

        p_vp = [p_o, p_v]

        def run(engine, slot):
            loop_from, loop_to = 2, NG // PAIR - 1
            for u in range(loop_from):
                for k in range(PAIR):
                    slot(Slot(u, k))
            with engine.Fori(loop_from, loop_to) as u:
                for k in range(PAIR):
                    slot(Slot(u, k))
            for k in range(PAIR * loop_to, NG + LAG_PV):
                slot(Slot(k // PAIR, k % PAIR))

        kh_dram, kl_dram = (k.rearrange("d (b k) -> b d k", k=S2) for k in (kh_dram, kl_dram))

        block = ctx.enter_context(nc.Block())

        @block.sync
        def _(sp):
            def load_kb(b):
                i = b.k // NCH % 2
                all_at_least(sp, (a_summed, b.over(NCH, -1, NCH * QT)))
                src = kh_dram[b.over(NCH)]
                for j in range(HC):
                    sp.dma_start(kb[i][DK * j:DK * (j + 1), :, S2 * j:S2 * (j + 1)].bitcast(F32),
                                 src.rearrange("(c j d) k -> j d c k", j=HC, d=DK)[j]).then_inc(kb_in[i], 16)

            def load_ks(b):
                i = b.k // NCH % 2
                all_at_least(sp, (s_summed, b.over(NCH, -1, NCH * HC)))
                for part, src in enumerate((kh_dram, kl_dram, kh_dram)):
                    sp.dma_start(ks[DK * part:DK * (part + 1), i, :, :].bitcast(F32),
                                 src[b.over(NCH)].rearrange("(h d) k -> d h k", d=DK)).then_inc(ks_in[i], 16)

            def load_v(b):
                i = b.k // NCH % 2
                if isinstance(b.u, int) and b.u == 0:
                    tiles = range(-(-S2 // P) if b.is_first() else VT)
                    for j in range(min(4, len(tiles))):
                        sp.wait_ge(v_stored[j], 16 * len(tiles[j::4]))
                all_at_least(sp, (pv_summed, b.over(NCH, -1, NCH)))
                sp.dma_start(vb[0:S2, i, :], v_dram[b.over(NCH)]).then_inc(vb_in[i], 16)

            def load_xt(n):
                all_at_least(sp, (xh_ready, n.over(1, -1)), (xl_ready, n.over(1, -1)))
                sp.dma_start(xt[:, n.k % 2, :], xt_dram[n.over(1)]).then_inc(xt_in[n.k % 2], 16)

            for n in range(KC, -LAG_LOAD_X):
                load_xt(Slot(0, n))

            def load_wo(kc):
                if kc >= 2:
                    sp.wait_ge(wo_high, kc - 1)
                    sp.wait_ge(wo_low, kc - 1)
                sp.dma_start(xn[:, kc % 2, :], a["Wo"][P * kc:P * (kc + 1), :]).then_inc(wo_in[kc % 2], 16)

            for kc in range(2):
                load_wo(kc)

            def store_v(i):
                r, n = tiles_v[i]
                sp.wait_ge(v_out, i + 1)
                sp.dma_start(v_dram.rearrange("b k d -> (b k) d")[r:r + n, :],
                             y[0:n, i % 4, :]).then_inc(v_stored[i % 4], 16)

            def slot(g):
                if g.k % 2 == 0 and g.back(2).valid(NG):
                    c = g.back(2)
                    i = c.k // 2 % 2
                    all_at_least(sp, (qh_ready, c.over(1, 2)), (ql_ready, c.over(1, 2)),
                                 (s_summed, c.over(2, -1, HALF)))
                    for part, src in enumerate((qh, qh, ql)):
                        for j in range(HC):
                            sp.dma_start(z[DK * part:DK * (part + 1), i, j::HC, :].bitcast(F32),
                                         src[DK * j:DK * (j + 1), i, :, :].bitcast(F32)).then_inc(z_in[i], 16)
                if g.k % NCH == 1 and g.valid(NG):
                    load_ks(g.back(1))
                if g.k % NCH == 3 and g.valid(NG):
                    load_v(g.back(3))
                if g.k % NCH == NCH - 1 and g.back(-1).valid(NG):
                    if g.back(NCH - 1).is_first():
                        sp.wait_ge(kb1_zeroed, 1)
                    load_kb(g.back(-1))
                if g.back(LAG_LOAD_X).valid(NG):
                    load_xt(g.back(LAG_LOAD_X))
                m = g.back(LAG_NORM - 2)
                if m.valid(NS):
                    if m.is_first():
                        sp.wait_ge(wo_low, KC)
                        sp.wait_ge(wo_high, KC)
                    all_at_least(sp, (y_ready, m.over(1, -1)))
                    sp.dma_start(xn[:, m.k % 2, :], x_dram[m.over(1)]).then_inc(xn_in[m.k % 2], 16)
                if last_batch_chunk(g, 1) == NCH - 1:
                    for t in range(QT):
                        if t == 0:
                            sp.wait_ge(xh_ready, NG)
                            sp.wait_ge(xl_ready, NG)
                        if t == 2:
                            sp.wait_ge(pv_summed, NG - NCH)
                        sp.dma_start(x_last[t], x_dram[NS + t]).then_inc(x_last_in[t], 16)
                if g.back(LAG_STORE).valid(NS):
                    store(g.back(LAG_STORE))
                for i in v_in_slot(g.back(1)):
                    store_v(i)
                if g.back(LAG_PV).is_first():
                    for row, src in ((gamma, "ln_gamma"), (beta, "ln_beta"), (bo, "bo")):
                        sp.dma_start(row[:], a[src].partition_broadcast(P)).then_inc(rows_in, 16)
                if g.back(LAG_PV + 1).is_first():
                    load_wo(2)
                    load_wo(3)

            def store(m):
                all_at_least(sp, (y_done, m.over(1, 1)))
                sp.dma_start(out_dram[m.over(1)], y[:, m.k % 4, :]).then_inc(stored[m.k % 4], 16)
            run(sp, slot)

            for m in range(NG + LAG_PV - LAG_STORE, NS):
                store(Slot(0, m))
            for t in (0, 2, 1, 3):
                if t < ON_POOL:
                    sp.wait_ge(y_done, NS + t + 1)
                else:
                    sp.wait_ge(y_last_done, t - ON_POOL + 1)
                sp.dma_start(out_dram[NS + t], x_last[t]).then_inc(stored[t], 16)
            for i in range(4):
                sp.wait_ge(stored[i], 16 * (NM // 4))

        @block.tensor
        def _(pe):
            def project_q(g, kc):
                i, c = g.k // NCH % 2, g.k % NCH
                if kc == 0:
                    if c == 0:
                        pe.wait_ge(xh_ready, g.over(NCH, 1, KC))
                        pe.wait_ge(xl_ready, g.over(NCH, 1, KC))
                    at_least(pe, ql_ready, g.over(1))
                for n, (w, x) in enumerate(((wqh, xh), (wqh, xl), (wql, xh))):
                    last = nc.tensor.matmul(p_q[:], w[:, kc, P * c:P * (c + 1)], x[:, i, kc, :],
                                            start=(kc == 0 and n == 0), stop=(kc == KC - 1 and n == 2))
                if kc == KC - 1:
                    last.then_inc(q_summed, 1)

            def rowmax_scores(g, t):
                if t == 0:
                    pe.wait_ge(qh_ready, g.over(1, 1))
                    if g.k % NCH == 0:
                        pe.wait_ge(kb_in[g.k // NCH % 2], g.over(PAIR, 1, 16 * KB_DMAS))
                if t < 2:
                    at_least(pe, max_ready, g.over(1, -1, QT) + t + 3)
                else:
                    pe.wait_ge(max_ready, g.over(1, 0, QT) + t - 1)
                s = g.back(LAG_SCORE - LAG_ROWMAX)
                if t == 1 and s.valid(NG):
                    pe.wait_ge(prob_ready, s.over(1, 0, HC) + HC - 1)
                nc.tensor.matmul(p_a[t % 2][:, 0:HC * S2], qh[:, g.k // 2 % 2, g.k % 2, P * t:P * (t + 1)],
                                 kb[g.k // NCH % 2][:, g.k % NCH, :], start=True, stop=True).then_inc(a_summed, 1)

            def turn_maxima(g):
                pe.wait_ge(max_ready, g.over(1, 2, QT))
                at_least(pe, shift_ready, g.over(2, 0, 2))
                for t in range(QT):
                    last = nc.tensor.transpose(p_t[0:HALF, P * t:P * (t + 1)], nm[:, g.k // 2 % 2, t, :], ident[:])
                last.then_inc(t_done, 1)

            def scores(g, j):
                i, s, h = g.k // 2 % 2, HC * (g.k % 2) + j, HC * (g.k % NCH) + j
                if j == 0:
                    if g.is_first():
                        pe.wait_ge(const_dve, 1)
                    pe.wait_ge(z_in[i], g.over(4, 1, 16 * Z_DMAS))
                    pe.wait_ge(shift_ready, g.over(1, 1))
                    if g.k % NCH == 0:
                        pe.wait_ge(ks_in[g.k // NCH % 2], g.over(PAIR, 1, 16 * KS_DMAS))
                at_least(pe, prob_ready, g.over(1, 0, HC) + j - 1)
                if j == 0:
                    newest = g.back(LAG_ROWMAX - LAG_SCORE + 1)
                    pe.wait_ge(max_ready, newest.over(1, 1, QT) if newest.valid(NG) else NG * QT)
                nc.tensor.matmul(p_s[j % 2][0:S2, :], ks[0:KR, g.k // NCH % 2, h, :], z[0:KR, i, s, :],
                                 start=True, stop=True).then_inc(s_summed, 1)

            def values(g):
                pe.wait_ge(prob_ready, g.over(1, 1, HC))
                if g.k % NCH == 0:
                    pe.wait_ge(vb_in[g.k // NCH % 2], g.over(PAIR, 1, 16))
                if g.is_first():
                    pe.wait_ge(v_out, VT)
                at_least(pe, cx_ready, g.over(1))
                for j in range(HC):
                    h = HC * (g.k % NCH) + j
                    nc.tensor.matmul(p_v[DK * j:DK * (j + 1), :], vb[0:S2, g.k // NCH % 2, DK * h:DK * (h + 1)],
                                     prob[0:S2, j, :], start=True, stop=True)
                for j in range(HC):
                    last = nc.tensor.matmul(p_d[DK * j:DK * (j + 1), :], ones[0:S2, :], prob[0:S2, j, :],
                                            start=True, stop=True)
                last.then_inc(pv_summed, 1)

            def project_out(m, kc):
                i, t = m.k // QT % 2, m.k % QT
                if kc == 0:
                    if m.is_first():
                        pe.wait_ge(wo_high, KC)
                        pe.wait_ge(wo_low, KC)
                    if t == 0:
                        pe.wait_ge(ch_ready, m.over(QT, 1, KC))
                        pe.wait_ge(cl_ready, m.over(QT, 1, KC))
                    at_least(pe, y_ready, m.over(1))
                for n, (x, w) in enumerate(((ch, woh), (ch, wol), (cl, woh))):
                    last = nc.tensor.matmul(p_o[:], x[:, i, kc, P * t:P * (t + 1)], w[:, kc, :],
                                            start=(kc == 0 and n == 0), stop=(kc == KC - 1 and n == 2))
                if kc == KC - 1:
                    last.then_inc(o_summed, 1)

            def project_last(c):
                pe.wait_ge(ch_ready, NG - NCH + c + 1)
                pe.wait_ge(cl_ready, NG - NCH + c + 1)
                steps = [(t, c) for t in range(QT - 1)]
                if c >= NCH - 2:
                    steps += [(QT - 1, kc) for kc in (range(NCH - 1) if c == NCH - 2 else (c,))]
                for t, kc in steps:
                    bank, left, count = last_banks[t]
                    if kc == 0:
                        pe.wait_ge(left, count)
                    for n, (x, w) in enumerate(((ch, woh), (ch, wol), (cl, woh))):
                        last = nc.tensor.matmul(bank[:], x[:, (B - 1) % 2, kc, P * t:P * (t + 1)], w[:, kc, :],
                                                start=(kc == 0 and n == 0), stop=(kc == KC - 1 and n == 2))
                    if kc == KC - 1:
                        last.then_inc(o_summed, 1)

            def slot(g):
                q, r, s, v, o = g, g.back(LAG_ROWMAX), g.back(LAG_SCORE), g.back(LAG_PV), g.back(LAG_OUT)
                if v.valid(NG):
                    values(v)
                if g.k % 2 == 1 and g.back(3).valid(NG):
                    turn_maxima(g.back(3))
                if s.valid(NG):
                    scores(s, 0)
                    scores(s, 1)
                parts = [(project_q, q, kc) for kc in range(KC) if q.valid(NG)]
                parts += [(project_out, o, kc) for kc in range(KC) if o.valid(NS)]
                if len(parts) == 2 * KC:
                    scores_after, maxima_after = (1, 3), (2, 4, 5, 6)
                elif s.valid(NG):
                    scores_after, maxima_after = (0, 1), (1, 2, 3, 3)
                else:
                    scores_after, maxima_after = (), (0, 1, 2, 3)
                for n, (project, chunk, kc) in enumerate(parts):
                    project(chunk, kc)
                    for j, after in enumerate(scores_after):
                        if s.valid(NG) and after == n:
                            scores(s, 2 + j)
                    for t, after in enumerate(maxima_after):
                        if r.valid(NG) and after == n:
                            rowmax_scores(r, t)
                for i in v_in_slot(g):
                    pe.wait_ge(v_out, i - 1)
                    r, n = tiles_v[i]
                    v_products(nc, keep, p_vp[i % 2], keep["cx2"], r - V_FIRST * P, n).then_inc(v_summed, 1)
                c = last_batch_chunk(g, LAG_PV + 1)
                if c is not None:
                    project_last(c)
            run(pe, slot)
            project_last(NCH - 1)

        @block.scalar
        def _(act):
            def exp(g, j):
                act.wait_ge(s_summed, g.over(1, 0, HC) + j + 1)
                if j == 0:
                    at_least(act, pv_summed, g.over(1))
                nc.scalar.activation(prob[0:S2, j, :], p_s[j % 2][0:S2, :], ACT.Exp, scale=SCALE).then_inc(prob_ready, 1)

            def split_x_high(n):
                i = n.k // KC % 2
                act.wait_ge(xt_in[n.k % 2], n.over(2, 1, 16))
                if n.k % KC == 0:
                    at_least(act, q_summed, n.over(KC, -1, NCH))
                nc.scalar.copy(xh[:, i, n.k % KC, :], xt[:, n.k % 2, :]).then_inc(xh_ready, 1)

            def place_maxima(g, cc):
                i = g.k // 2 % 2
                if cc == 0:
                    act.wait_ge(t_done, g.over(2, 1))
                    at_least(act, s_summed, g.over(2, -1, HALF))
                nc.scalar.copy(z[QI:KR, i, HC * cc:HC * (cc + 1), :],
                               p_t[0:HALF, :].unsqueeze(1).broadcast_to([HALF, HC, S])).then_inc(shift_ready, 1)

            def q_high(g):
                i = g.k // 2 % 2
                act.wait_ge(q_summed, g.over(1, 1))
                at_least(act, a_summed, g.over(1, -3, QT))
                if g.k % 2 == 0:
                    at_least(act, z_in[i], g.over(4, 0, 16 * Z_DMAS))
                nc.scalar.activation(qh[:, i, g.k % 2, :], p_q[:], ACT.Identity,
                                     bias=bq_col[:, g.k % NCH:g.k % NCH + 1]).then_inc(qh_ready, 1)

            def ctx_high(g):
                i = g.k // NCH % 2
                act.wait_ge(cx_ready, g.over(1, 1))
                if g.is_first():
                    act.wait_ge(v_summed, VT)
                if g.k % NCH == 0:
                    at_least(act, o_summed, g.over(NCH, -1, QT))
                nc.scalar.copy(ch[:, i, g.k % NCH, :], cx[:, g.k % 2, :]).then_inc(ch_ready, 1)

            def normalize(m):
                i = m.k % 4
                act.wait_ge(nmr_ready, m.over(1, 1))
                nc.scalar.activation(rows(m), rows(m), ACT.Identity, bias=nmr[:, i, :],
                                     scale=rstd[:, i, :]).then_inc(normed, 1)

            def split_wo_high(kc):
                act.wait_ge(wo_in[kc % 2], 16 * (kc // 2 + 1))
                act.wait_ge(v_summed, VT)
                nc.scalar.copy(keep["woh"][:, kc, :], xn[:, kc % 2, :]).then_inc(wo_high, 1)

            act.wait_ge(keep["bq_in"], 16)

            def is_short(g):
                return not g.back(LAG_OUT).valid(NS) or not g.valid(NG)

            def leaves_maxima(g):
                return is_short(g) or not g.back(-1).valid(NG)

            def slot(g):
                s, v, m, n = g.back(LAG_SCORE), g.back(LAG_PV), g.back(LAG_NORM), g.back(LAG_SPLIT)
                turn = g.k % 2 == 1 and g.back(3).valid(NG)
                short = is_short(g)
                late_maxima = g.k % 2 == 0 and g.back(4).valid(NG) and leaves_maxima(g.back(1))
                if s.valid(NG):
                    exp(s, 0)
                    exp(s, 1)
                if n.valid(NG):
                    split_x_high(n)
                if s.valid(NG):
                    exp(s, 2)
                if s.valid(NG) and short:
                    exp(s, 3)
                if turn and short:
                    place_maxima(g.back(3), 0)
                if late_maxima:
                    place_maxima(g.back(4), 1)
                if g.valid(NG):
                    q_high(g)
                if s.valid(NG) and not short:
                    exp(s, 3)
                if turn and not short:
                    place_maxima(g.back(3), 0)
                if v.valid(NG):
                    ctx_high(v)
                if m.valid(NS):
                    normalize(m)
                if turn and not leaves_maxima(g):
                    place_maxima(g.back(3), 1)
                for kc in wo_in_slot(g):
                    split_wo_high(kc)
            run(act, slot)
            for m in range(NG + LAG_PV - LAG_NORM, NS + ON_POOL):
                normalize(Slot(0, m))

        @block.vector
        def _(dve):
            for i in range(2):
                for hf in range(2):
                    last = nc.vector.tensor_copy(ks[QI:KR, i, HALF * hf:HALF * (hf + 1), :],
                                                 ident[0:HALF, 0:HALF].unsqueeze(2).broadcast_to([HALF, HALF, S2]))
            last.then_inc(const_dve, 1)

            dve.wait_ge(keep["bq_in"], 16)

            def add_residual(m):
                i = m.k % 4
                dve.wait_ge(o_summed, m.over(1, 1))
                dve.wait_ge(xb_ready, m.over(1, 1))
                at_least(dve, stored[i], m.over(4, 0, 16))
                nc.vector.tensor_tensor(y[:, i, :], p_o[:], xn[:, m.k % 2, :], ALU.add).then_inc(y_ready, 1)
                dve.wait_ge(y_ready, m.over(1, 1))
                nc.vector.bn_stats(stats[:, i, :], y[:, i, :]).then_inc(stats_ready, 1)

            def invert_sums(g):
                dve.wait_ge(pv_summed, g.over(1, 1))
                nc.vector.reciprocal(rden[:], p_d[:]).then_inc(rden_ready, 1)

            def variance(m):
                i = m.k % 4
                nc.vector.bn_aggr(mv[:, i, :], stats[:, i, :]).then_inc(mv_ready, 1)
                dve.wait_ge(mv_ready, m.over(1, 1))
                nc.vector.tensor_scalar(ve[:, i, :], mv[:, i, 1:2], EPS, None, ALU.add).then_inc(ve_ready, 1)

            def divide(g):
                i = g.k % 2
                dve.wait_ge(rden_ready, g.over(1, 1))
                at_least(dve, ch_ready, g.over(1, -1))
                at_least(dve, cl_ready, g.over(1, -1))
                nc.vector.tensor_tensor(cx[:, i, :], p_v[:], rden[:], ALU.mult).then_inc(cx_ready, 1)

            def mean_over_std(m):
                i = m.k % 4
                dve.wait_ge(rstd_ready, m.over(1, 1))
                nc.vector.scalar_tensor_tensor(out=nmr[:, i, :], in0=mv[:, i, 0:1], scalar=-1.0, in1=rstd[:, i, :],
                                               op0=ALU.mult, op1=ALU.mult).then_inc(nmr_ready, 1)

            def q_low(g):
                i = g.k // 2 % 2
                dve.wait_ge(qh_ready, g.over(1, 1))
                if g.k % 2 == 0:
                    at_least(dve, z_in[i], g.over(4, 0, 16 * Z_DMAS))
                nc.vector.scalar_tensor_tensor(
                    out=ql[:, i, g.k % 2, :], in0=p_q[:], scalar=bq_col[:, g.k % NCH:g.k % NCH + 1],
                    in1=qh[:, i, g.k % 2, :].bitcast(F32), op0=ALU.add, op1=ALU.subtract).then_inc(ql_ready, 1)

            def row_maxima(g, t):
                i = g.k // 2 % 2
                dve.wait_ge(a_summed, g.over(1, 0, QT) + t + 1)
                if t == 0 and g.k % 2 == 0:
                    at_least(dve, t_done, g.over(2, -1))
                nc.vector.tensor_reduce(nm[:, i, t, HC * (g.k % 2):HC * (g.k % 2 + 1)],
                                        p_a[t % 2][:, 0:HC * S2].rearrange("p (h k) -> p h k", k=S2),
                                        AX_X, ALU.max, negate=True).then_inc(max_ready, 1)

            def slot(g):
                r, v, m = g.back(LAG_ROWMAX), g.back(LAG_PV), g.back(LAG_NORM)
                if m.valid(NS):
                    add_residual(m)
                    dve.wait_ge(stats_ready, m.over(1, 1))
                if v.valid(NG):
                    invert_sums(v)
                spread = not g.back(LAG_OUT).valid(NS)
                for t in range(2 if spread else 1):
                    if r.valid(NG):
                        row_maxima(r, t)
                if v.valid(NG):
                    divide(v)
                if m.valid(NS):
                    variance(m)
                if r.valid(NG) and not spread:
                    row_maxima(r, 1)
                if g.valid(NG) and not spread:
                    q_low(g)
                if r.valid(NG):
                    row_maxima(r, 2)
                    row_maxima(r, 3)
                if g.valid(NG) and spread:
                    q_low(g)
                if m.valid(NS):
                    mean_over_std(m)
                for i in v_in_slot(g):
                    dve.wait_ge(v_summed, i + 1)
                    dve.wait_ge(v_stored[i % 4], 16 * (i // 4))
                    n = tiles_v[i][1]
                    nc.vector.tensor_tensor(y[0:n, i % 4, :], p_vp[i % 2][0:n, :], bv_row[0:n, :],
                                            ALU.add).then_inc(v_out, 1)
            run(dve, slot)

            def add_last(t):
                dve.wait_ge(o_summed, NS + t + 1)
                dve.wait_ge(xb_last_ready, t + 1)
                nc.vector.tensor_tensor(x_last[t], last_banks[t][0][:], x_last[t], ALU.add).then_inc(y_ready, 1)
                dve.wait_ge(y_ready, NS + t + 1)
                nc.vector.bn_stats(stats[:, t, :], x_last[t]).then_inc(stats_ready, 1)
                dve.wait_ge(stats_ready, NS + t + 1)
                variance(Slot(0, NS + t))

            def center_scale(t):
                nc.vector.scalar_tensor_tensor(out=x_last[t], in0=x_last[t], scalar=mv[:, t, 0:1], in1=gamma[:],
                                               op0=ALU.subtract, op1=ALU.mult).then_inc(y_last_scaled, 1)

            def divide_shift(t):
                dve.wait_ge(rstd_ready, NS + t + 1)
                dve.wait_ge(y_last_scaled, t - ON_POOL + 1)
                nc.vector.scalar_tensor_tensor(out=x_last[t], in0=x_last[t], scalar=rstd[:, t, :], in1=beta[:],
                                               op0=ALU.mult, op1=ALU.add).then_inc(y_last_done, 1)

            m = Slot(0, NS - 1)
            add_residual(m)
            dve.wait_ge(stats_ready, NS)
            variance(m)
            add_last(0)
            mean_over_std(m)
            add_last(1)
            mean_over_std(Slot(0, NS))
            add_last(2)
            mean_over_std(Slot(0, NS + 1))
            center_scale(2)
            add_last(3)
            divide_shift(2)
            center_scale(3)
            divide_shift(3)

        @block.gpsimd
        def _(pool):
            nc.gpsimd.memset(kb[1][:].bitcast(F32), 0.0).then_inc(kb1_zeroed, 1)

            def split_x_low(n):
                i = n.k // KC % 2
                pool.wait_ge(xh_ready, n.over(1, 1))
                nc.gpsimd.tensor_tensor(xl[:, i, n.k % KC, :], xt[:, n.k % 2, :],
                                        xh[:, i, n.k % KC, :].bitcast(F32), ALU.subtract).then_inc(xl_ready, 1)

            def inverse_std(m):
                i = m.k % 4
                pool.wait_ge(ve_ready, m.over(1, 1))
                nc.gpsimd.tensor_tensor(rstd[:, i, :], ve[:, i, :], minus_half[:], ALU.pow).then_inc(rstd_ready, 1)

            def scale(m):
                pool.wait_ge(normed, m.over(1, 1))
                nc.gpsimd.tensor_tensor(rows(m), rows(m), gamma[:], ALU.mult).then_inc(scaled, 1)

            def shift(m):
                pool.wait_ge(scaled, m.over(1, 1))
                nc.gpsimd.tensor_tensor(rows(m), rows(m), beta[:], ALU.add).then_inc(y_done, 1)

            def ctx_low(g):
                i = g.k // NCH % 2
                pool.wait_ge(ch_ready, g.over(1, 1))
                nc.gpsimd.tensor_tensor(cl[:, i, g.k % NCH, :], cx[:, g.k % 2, :],
                                        ch[:, i, g.k % NCH, :].bitcast(F32), ALU.subtract).then_inc(cl_ready, 1)

            def add_bo(m):
                if m.is_first():
                    pool.wait_ge(rows_in, 48)
                pool.wait_ge(xn_in[m.k % 2], m.over(2, 1, 16))
                nc.gpsimd.tensor_tensor(xn[:, m.k % 2, :], xn[:, m.k % 2, :], bo[:], ALU.add).then_inc(xb_ready, 1)

            def add_bo_last(t):
                pool.wait_ge(x_last_in[t], 16)
                nc.gpsimd.tensor_tensor(x_last[t], x_last[t], bo[:], ALU.add).then_inc(xb_last_ready, 1)

            def slot(g):
                v, m, n, b = g.back(LAG_PV), g.back(LAG_NORM), g.back(LAG_SPLIT), g.back(LAG_NORM - 1)
                if g.back(LAG_SCALE).valid(NS):
                    scale(g.back(LAG_SCALE))
                    shift(g.back(LAG_SCALE))
                if n.valid(NG):
                    split_x_low(n)
                if b.valid(NS):
                    add_bo(b)
                if m.valid(NS):
                    inverse_std(m)
                if v.valid(NG):
                    ctx_low(v)
                t = last_batch_chunk(g, LAG_PV)
                if t is not None:
                    add_bo_last(t)
                for kc in wo_in_slot(g):
                    pool.wait_ge(wo_high, kc + 1)
                    nc.gpsimd.tensor_tensor(keep["wol"][:, kc, :], xn[:, kc % 2, :],
                                            keep["woh"][:, kc, :].bitcast(F32), ALU.subtract).then_inc(wo_low, 1)
            run(pool, slot)

            last = [Slot(0, NS + t) for t in range(-2, QT)]
            scale(last[0])
            inverse_std(last[1])
            shift(last[0])
            inverse_std(last[2])
            scale(last[1])
            inverse_std(last[3])
            shift(last[1])
            inverse_std(last[4])
            scale(last[2])
            inverse_std(last[5])
            shift(last[2])
            scale(last[3])
            shift(last[3])


def xattn(nc, a, out):
    B, S, _ = a["x"].shape
    S2 = a["ctx_t"].shape[1] // B
    kh_dram = nc.dram_tensor("k_high", (D, B * S2), F32, kind="Internal").ap()
    kl_dram = nc.dram_tensor("k_low", (D, B * S2), F32, kind="Internal").ap()
    v_dram = nc.dram_tensor("v_all", (B, S2, D), F32, kind="Internal").ap()
    with ExitStack() as ctx:
        keep = {n: ctx.enter_context(nc.sbuf_tensor(n, [P, KC, D], F32R)) for n in ("wqh", "wql", "woh", "wol")}
        for n, shape, dt in (("bq_col", [P, KC], F32),
                             ("xt", [P, 2, S], F32),
                             ("xh", [P, 2, KC, S], F32R),
                             ("xl", [P, 2, KC, S], F32R),
                             ("y", [P, 4, D], F32),
                             ("kb0", [P, NCH, HC * S2], F32R),
                             ("bv_row", [P, D], F32),
                             ("ident", [P, P], F32), ("ones", [P, DK], F32), ("minus_half", [P, 1], F32)):
            keep[n] = ctx.enter_context(nc.sbuf_tensor(n, shape, dt))
        keep["wvh"], keep["wvl"] = keep["woh"], keep["wol"]
        n2, part = B * S2 - V_FIRST * P, 2 * KC * S
        assert n2 <= 2 * S
        for n in ("ch", "cl"):
            buffer = ctx.enter_context(nc.sbuf_tensor(n, [P, part], F32R))
            keep[n] = buffer[:].rearrange("p (b c s) -> p b c s", b=2, c=KC)
            keep.setdefault("cx2", []).append(buffer[:, 0:KC * n2].rearrange("p (c n) -> p c n", c=KC))
        for n in ("bq_in", "xh_ready", "xl_ready", "const_pool", "kb0_zeroed", "v_summed", "v_out"):
            keep[n] = ctx.enter_context(nc.semaphore(n))
        for n, count in (("xt_in", 2), ("v_stored", 4), ("kb_in", 2)):
            keep[n] = [ctx.enter_context(nc.semaphore(f"{n}{i}")) for i in range(count)]
        project_context(nc, a, keep, kh_dram, kl_dram, v_dram.rearrange("b k d -> (b k) d"), B, S2)
        attend(nc, a, keep, kh_dram, kl_dram, v_dram, out, B, S, S2)


def kernel(**inputs):
    import numpy as np
    import concourse.bacc as bacc
    from concourse.bass_utils import run_bass_kernel_spmd

    x = np.ascontiguousarray(inputs["x"])
    context = np.asarray(inputs["ctx_1024"])
    w = {n: np.asarray(inputs[f"L0_xattn_{n}"])
         for n in ("Wq", "bq", "Wk", "bk", "Wv", "bv", "Wo", "bo", "ln_gamma", "ln_beta")}
    arrays = {"x": x, "x_t": np.ascontiguousarray(x.transpose(0, 2, 1)),
              "ctx_t": np.ascontiguousarray(context.reshape(-1, D).T)}
    for n, v in w.items():
        arrays[n] = np.ascontiguousarray(v.reshape(KC, P).T if n in ("bq", "bk") else v)
    nc = bacc.Bacc("TRN2", target_bir_lowering=False, num_devices=1)
    a = {n: nc.dram_tensor(f"in_{n}", v.shape, mybir.dt.from_np(v.dtype), kind="ExternalInput").ap()
         for n, v in arrays.items()}
    out = nc.dram_tensor("out_0_dram", x.shape, F32, kind="ExternalOutput").ap()
    xattn(nc, a, out)
    r = run_bass_kernel_spmd(nc, [{f"in_{n}": v for n, v in arrays.items()}], core_ids=[0])
    return r.results[0]["out_0_dram"]
```
